# Optimizing a Trainium2 kernel written in Bass

```python
import numpy as np
import jax
import jax.numpy as jnp

def _softmax(x, axis=-1):
    return jax.nn.softmax(x, axis=axis)

def _gelu(x):
    return jax.nn.gelu(x, approximate=True)

def _silu(x):
    return jax.nn.silu(x)

def _sigmoid(x):
    return jax.nn.sigmoid(x)

def _layernorm(x, axis=-1, eps=1e-05):
    m = jnp.mean(x, axis=axis, keepdims=True)
    v = jnp.var(x, axis=axis, keepdims=True)
    return (x - m) / jnp.sqrt(v + eps)

def _scatter_add(tgt, idx, src, axis=0):
    return tgt.at[idx].add(src)

def _segment_sum(src, seg, n):
    return jax.ops.segment_sum(src, seg, n)
kernel_name = 'mk_conv_preact_d2_conv_nhwc384_r4_37ca4e'

def setup_inputs(seed: int=0):
    np.random.seed(seed)
    _w = jnp.asarray

    def _rec_inputs():
        import jax
        import jax.numpy as jnp
        _gk = jax.random.key(seed)
        x = -0.0001476 + 0.9999 * jax.random.normal(jax.random.fold_in(_gk, 1), (32, 56, 56, 96), jnp.float32)
        return x
    x = _rec_inputs()

    def _L0_conv_setup():
        import jax, jax.numpy as jnp
        import numpy as np
        WIN = 7
        SHIFT = 3
        HEADS = 12
        L = WIN * WIN

        def _relative_position_index():
            coords = np.stack(np.meshgrid(np.arange(WIN), np.arange(WIN), indexing='ij'))
            flat = coords.reshape(2, -1)
            rel = flat[:, :, None] - flat[:, None, :]
            rel = rel.transpose(1, 2, 0).astype(np.int64)
            rel[..., 0] += WIN - 1
            rel[..., 1] += WIN - 1
            rel[..., 0] *= 2 * WIN - 1
            return rel.sum(-1).reshape(-1)

        def _shift_mask(H, W):
            img = np.zeros((H, W), dtype=np.float32)
            slices = [(0, -WIN), (-WIN, -SHIFT), (-SHIFT, None)]
            cnt = 0
            for hs in slices:
                for ws in slices:
                    img[hs[0]:hs[1], ws[0]:ws[1]] = cnt
                    cnt += 1
            nH, nW = (H // WIN, W // WIN)
            mw = img.reshape(nH, WIN, nW, WIN).transpose(0, 2, 1, 3).reshape(nH * nW, L)
            diff = mw[:, :, None] - mw[:, None, :]
            return np.where(diff != 0, -100.0, 0.0).astype(np.float32)
        key = jax.random.key(seed)
        ks = jax.random.split(key, 6)
        C = 96
        return {'x': jax.random.normal(ks[0], (32, 56, 56, C), dtype=jnp.float32), 'qkv_w': jax.random.normal(ks[1], (3 * C, C), dtype=jnp.float32) * 0.02, 'qkv_b': jax.random.normal(ks[2], (3 * C,), dtype=jnp.float32) * 0.02, 'proj_w': jax.random.normal(ks[3], (C, C), dtype=jnp.float32) * 0.02, 'proj_b': jax.random.normal(ks[4], (C,), dtype=jnp.float32) * 0.02, 'rel_table': jax.random.normal(ks[5], ((2 * WIN - 1) ** 2, HEADS), dtype=jnp.float32) * 0.02}
    _L0_conv_all = _L0_conv_setup()
    _L0_conv_in = {k: v for k, v in _L0_conv_all.items() if k in ('qkv_w', 'qkv_b', 'proj_w', 'proj_b', 'rel_table')}
    del _L0_conv_all

    def _L1_conv_setup():
        import jax, jax.numpy as jnp
        import numpy as np
        WINDOW = (1, 5, 20)
        FILL = 1.0

        def box_sum(x, axis, w):
            if w == 1:
                return x
            lo = w // 2
            hi = w - lo - 1
            xm = jnp.moveaxis(x, axis, -1)
            shp = xm.shape
            xr = xm.reshape(-1, 1, shp[-1])
            k = jnp.ones((1, 1, w), x.dtype)
            y = jax.lax.conv_general_dilated(xr, k, window_strides=(1,), padding=[(lo, hi)])
            return jnp.moveaxis(y.reshape(shp), -1, axis)
        key = jax.random.key(seed)
        x = jax.random.normal(key, (2, 64, 64, 96), dtype=jnp.float32)
        return {'x': x}
    _L1_conv_all = _L1_conv_setup()
    _L1_conv_in = {k: v for k, v in _L1_conv_all.items() if k in ()}
    del _L1_conv_all
    return {'x': x, 'L0_conv_qkv_w': _L0_conv_in['qkv_w'], 'L0_conv_qkv_b': _L0_conv_in['qkv_b'], 'L0_conv_proj_w': _L0_conv_in['proj_w'], 'L0_conv_proj_b': _L0_conv_in['proj_b'], 'L0_conv_rel_table': _L0_conv_in['rel_table']}

def reference(x, L0_conv_qkv_w, L0_conv_qkv_b, L0_conv_proj_w, L0_conv_proj_b, L0_conv_rel_table):
    import jax
    import jax.numpy as jnp

    def _L0_conv_ref(x, qkv_w, qkv_b, proj_w, proj_b, rel_table):
        import jax, jax.numpy as jnp
        import numpy as np
        WIN = 7
        SHIFT = 3
        HEADS = 12
        L = WIN * WIN

        def _relative_position_index():
            coords = np.stack(np.meshgrid(np.arange(WIN), np.arange(WIN), indexing='ij'))
            flat = coords.reshape(2, -1)
            rel = flat[:, :, None] - flat[:, None, :]
            rel = rel.transpose(1, 2, 0).astype(np.int64)
            rel[..., 0] += WIN - 1
            rel[..., 1] += WIN - 1
            rel[..., 0] *= 2 * WIN - 1
            return rel.sum(-1).reshape(-1)

        def _shift_mask(H, W):
            img = np.zeros((H, W), dtype=np.float32)
            slices = [(0, -WIN), (-WIN, -SHIFT), (-SHIFT, None)]
            cnt = 0
            for hs in slices:
                for ws in slices:
                    img[hs[0]:hs[1], ws[0]:ws[1]] = cnt
                    cnt += 1
            nH, nW = (H // WIN, W // WIN)
            mw = img.reshape(nH, WIN, nW, WIN).transpose(0, 2, 1, 3).reshape(nH * nW, L)
            diff = mw[:, :, None] - mw[:, None, :]
            return np.where(diff != 0, -100.0, 0.0).astype(np.float32)
        N, H, W, C = x.shape
        d = C // HEADS
        nH, nW = (H // WIN, W // WIN)
        num_win = nH * nW
        idx = _relative_position_index()
        bias = rel_table[idx].reshape(L, L, HEADS).transpose(2, 0, 1)
        xs = jnp.roll(x, shift=(-SHIFT, -SHIFT), axis=(1, 2))
        xw = xs.reshape(N, nH, WIN, nW, WIN, C).transpose(0, 1, 3, 2, 4, 5)
        xw = xw.reshape(N * num_win, L, C)
        qkv = xw @ qkv_w.T + qkv_b
        qkv = qkv.reshape(N * num_win, L, 3, HEADS, d).transpose(2, 0, 3, 1, 4)
        q, k, v = (qkv[0], qkv[1], qkv[2])
        q = q * d ** (-0.5)
        attn = jnp.einsum('bhqd,bhkd->bhqk', q, k) + bias[None]
        mask = jnp.asarray(_shift_mask(H, W))
        attn = attn.reshape(N, num_win, HEADS, L, L) + mask[None, :, None]
        attn = attn.reshape(N * num_win, HEADS, L, L)
        attn = jax.nn.softmax(attn, axis=-1)
        out = jnp.einsum('bhqk,bhkd->bhqd', attn, v)
        out = out.transpose(0, 2, 1, 3).reshape(N * num_win, L, C)
        out = out @ proj_w.T + proj_b
        out = out.reshape(N, nH, nW, WIN, WIN, C).transpose(0, 1, 3, 2, 4, 5)
        out = out.reshape(N, H, W, C)
        out = jnp.roll(out, shift=(SHIFT, SHIFT), axis=(1, 2))
        return out

    def _L1_conv_ref(x):
        import jax, jax.numpy as jnp
        import numpy as np
        WINDOW = (1, 5, 20)
        FILL = 1.0

        def box_sum(x, axis, w):
            if w == 1:
                return x
            lo = w // 2
            hi = w - lo - 1
            xm = jnp.moveaxis(x, axis, -1)
            shp = xm.shape
            xr = xm.reshape(-1, 1, shp[-1])
            k = jnp.ones((1, 1, w), x.dtype)
            y = jax.lax.conv_general_dilated(xr, k, window_strides=(1,), padding=[(lo, hi)])
            return jnp.moveaxis(y.reshape(shp), -1, axis)
        w0, w1, w2 = WINDOW
        s = box_sum(box_sum(x, 1, w0), 2, w1)
        num = box_sum(s * s, 3, w2)
        d = box_sum(box_sum(box_sum(x * x, 1, w0), 2, w1), 3, w2)
        c0 = box_sum(jnp.ones((x.shape[1],), x.dtype), 0, w0)
        c1 = box_sum(jnp.ones((x.shape[2],), x.dtype), 0, w1)
        norm = c0[:, None] * c1[None, :]
        denum = d * norm[None, :, :, None]
        return jnp.nan_to_num(num / denum, nan=FILL)

    def _gn(v, G=32, eps=1e-05):
        B_, H_, W_, C_ = v.shape
        g = v.reshape(B_, H_, W_, G, C_ // G)
        m = jnp.mean(g, axis=(1, 2, 4), keepdims=True)
        s = jnp.var(g, axis=(1, 2, 4), keepdims=True)
        return ((g - m) / jnp.sqrt(s + eps)).reshape(v.shape)

    def _ln_c(v, eps=1e-06):
        m = jnp.mean(v, axis=-1, keepdims=True)
        s = jnp.var(v, axis=-1, keepdims=True)
        return (v - m) / jnp.sqrt(s + eps)

    def _ln_t(v, eps=1e-05):
        m = jnp.mean(v, axis=-1, keepdims=True)
        s = jnp.var(v, axis=-1, keepdims=True)
        return (v - m) / jnp.sqrt(s + eps)

    def _to_tokens(v):
        B_, H_, W_, C_ = v.shape
        return v.reshape(B_, H_ * W_, C_)

    def _from_tokens(t, like):
        return t.reshape(like.shape)
    x = x + _L0_conv_ref(_gn(x), L0_conv_qkv_w, L0_conv_qkv_b, L0_conv_proj_w, L0_conv_proj_b, L0_conv_rel_table)
    x = x + _L1_conv_ref(_gn(x))
    return x

_drawn_inputs = setup_inputs


def setup_inputs(seed=0):
    import zlib

    import numpy as np

    out = dict(_drawn_inputs(seed))
    spreads = {}
    factors = {'L0_conv_qkv_w': 8.0,
     'L0_conv_qkv_b': 8.0,
     'L0_conv_proj_w': 7.848,
     'L0_conv_proj_b': 2.868,
     'L0_conv_rel_table': 8.0}
    for name, (base, spread) in spreads.items():
        noise = np.random.default_rng([zlib.crc32(name.encode()), seed]).standard_normal(out[name].shape)
        drawn = base * np.exp(spread * noise) if base else spread * noise
        out[name] = jnp.asarray(drawn.astype(out[name].dtype))
    for name, factor in factors.items():
        out[name] = (out[name] * factor).astype(out[name].dtype)
    return out
```

```python
from contextlib import ExitStack

import numpy as np

import concourse.bass as bass
from concourse import mybir

F32 = mybir.dt.float32
BF16 = mybir.dt.bfloat16
ALU = mybir.AluOpType
ACT = mybir.ActivationFunctionType
AX = mybir.AxisListType

IMAGES, SIDE, C = 32, 56, 96
WIN, SHIFT, HEADS = 7, 3, 12
L = WIN * WIN
D = C // HEADS
UNITS = SIDE // WIN
PAIRS = SIDE // WIN // 2
STEPS = UNITS * PAIRS
TOK = UNITS * L
HQ = 4
HG = HEADS // HQ
HP = HEADS // 2
HALF = HEADS // 2 * L
SC = HEADS * L
VC = 2 * 2 * (D + 1)
PW = 64
LEFT = 2
GRP = 3
EPS = 1e-5
TINY = 1e-36

K_ID, K_ROLL, K_BAND, K_GRP = 0, 128, 240, 336
K_MASK = 432
K_HALF = K_MASK + 4 * L
K_N = K_HALF + 2


def shape_constants():
    k = np.zeros((128, K_N), np.float32)
    k[:, K_ID:K_ID + 128] = np.eye(128)
    for j in range(2 * SIDE):
        k[j // SIDE * SIDE + (j % SIDE + SHIFT) % SIDE, K_ROLL + j] = 1
    for c in range(C):
        k[max(0, c - 10):min(C, c + 10), K_BAND + c] = 1
        k[c // GRP * GRP:(c // GRP + 1) * GRP, K_GRP + c] = 1.0 / GRP
    t = np.arange(L)
    region = [t // WIN >= WIN - SHIFT, t % WIN >= WIN - SHIFT]
    for last_row in range(2):
        for last_col in range(2):
            for w in range(2):
                cut = np.zeros((L, L), bool)
                if last_row:
                    cut |= region[0][:, None] != region[0][None, :]
                if last_col and w == 1:
                    cut |= region[1][:, None] != region[1][None, :]
                at = K_MASK + (2 * last_row + last_col) * L
                k[64 * w:64 * w + L, at:at + L] = np.where(cut, -100.0, 0.0)
    for h in range(2):
        k[64 * h:64 * h + L, K_HALF + h] = 1
    return k


class Signal:

    def __init__(self, sem, per, first=0):
        self.sem, self.per, self.first = sem, per, first

    def at(self, image, k):
        return image * self.per + (self.first + k)


def build(nc, x, wT, bias_row, pT, pb_row, flipped, consts, out):
    ctx = ExitStack()
    with ctx:
        def sb(name, shape, dt=F32):
            return ctx.enter_context(nc.sbuf_tensor(name, shape, dt))

        def psum(name, shape):
            return ctx.enter_context(nc.psum_tensor(name, shape, F32))

        def signal(name, per, first=0):
            return Signal(ctx.enter_context(nc.semaphore(name)), per, first)

        K = sb("K", [128, K_N])
        ident = K[:, K_ID:K_ID + 128]
        roll = K[:, K_ROLL:K_ROLL + 2 * SIDE]
        band = K[0:C, K_BAND:K_BAND + C]
        group = K[0:C, K_GRP:K_GRP + C]
        half_of = K[:, K_HALF:K_HALF + 2]
        WT = sb("WT", [C + 1, 3 * C])
        W32 = sb("W32", [C + 1, 3 * C])
        WH = sb("WH", [C + 1, 3 * C], BF16)
        WL = sb("WL", [C + 1, 3 * C], BF16)
        PT = sb("PT", [C + 1, C])
        PH = sb("PH", [C + 1, C], BF16)
        PL = sb("PL", [C + 1, C], BF16)
        bias_raw = sb("bias_raw", [128, L, HEADS])
        table = [sb(f"table{i}", [128, SC]) for i in range(4)]

        LOADS = 4
        tok_in = [sb(f"tok_in{i}", [2 * SIDE, 4, C]) for i in range(LOADS)]
        X = sb("X", [C, UNITS * TOK])
        XH = sb("XH", [C + 1, UNITS * TOK + 16], BF16)
        XL = sb("XL", [C + 1, UNITS * TOK + 16], BF16)
        qn = [[sb(f"qn{p}{i}", [C, 2 * TOK], BF16) for i in range(2)] for p in "hl"]
        kn = [[sb(f"kn{p}{i}", [C, 2 * TOK], BF16) for i in range(2)] for p in "hl"]
        QS = [sb(f"QS{i}", [128, HG, 2 * TOK + 16], BF16) for i in range(2)]
        KS = sb("KS", [128, HG, 2 * TOK], BF16)
        KE = [sb(f"KE{i}", [128, HEADS, 2 * TOK], BF16) for i in range(2)]
        VH = [sb(f"VH{i}", [128, PAIRS * HP, 2, 2, D + 1], BF16) for i in range(2)]
        VL = [sb(f"VL{i}", [128, PAIRS * HP, 2, 2, D + 1], BF16) for i in range(2)]
        T = [sb(f"T{i}", [128, HEADS, 64]) for i in range(2)]
        MX = [sb(f"MX{i}", [128, HEADS]) for i in range(2)]
        P32 = [sb(f"P32{i}", [128, HEADS, L]) for i in range(2)]
        PRH = [sb(f"PRH{i}", [128, HEADS, 64], BF16) for i in range(4)]
        PRL = [sb(f"PRL{i}", [128, HEADS, 64], BF16) for i in range(4)]
        rden = sb("rden", [128, 2 * HP, 2, 2])
        O = [sb(f"O{i}", [128, PAIRS, C]) for i in range(2)]
        OH = sb("OH", [C + 1, TOK], BF16)
        OL = sb("OL", [C + 1, TOK], BF16)
        X1 = sb("X1", [C, SIDE, PW])
        Y = [sb(f"Y{i}", [C, WIN, PW]) for i in range(2)]
        SQ = [sb(f"SQ{i}", [C, WIN, PW]) for i in range(2)]
        y2 = sb("y2", [C, WIN, PW])
        y4 = sb("y4", [C, WIN, PW])
        q2 = sb("q2", [C, WIN, PW])
        q4 = sb("q4", [C, WIN, PW])
        ybox = [sb(f"ybox{i}", [C, WIN, SIDE]) for i in range(2)]
        qbox = [sb(f"qbox{i}", [C, WIN, SIDE]) for i in range(2)]
        ybox2 = [sb(f"ybox2{i}", [C, WIN, SIDE]) for i in range(2)]
        lnd = sb("lnd", [C, TOK])
        rd0 = [sb(f"rd0{i}", [C, TOK]) for i in range(2)]
        de = sb("de", [C, TOK])
        nu = sb("nu", [C, TOK])
        ra = sb("ra", [C, TOK])
        res = [sb(f"res{i}", [C, TOK + SIDE]) for i in range(2)]
        tok_out = [sb(f"tok_out{i}", [2 * SIDE, 4, C]) for i in range(4)]
        stats = [sb(f"stats{i}", [C, UNITS, 6]) for i in range(2)]
        mv = [sb(f"mv{i}", [C, 2]) for i in range(2)]
        g = [sb(f"g{i}", [C, 13]) for i in range(2)]
        DEV, V2, VE, LN, R0, SQR, SQV, NW, RS, NB, RS5, NB5, GATE = range(13)
        tiny = sb("tiny", [C, 1])

        pS = psum("pS", [128, 2, 512])
        pP = psum("pP", [128, 2, 512])
        pO = psum("pO", [128, 512])
        pM = [psum(f"pM{i}", [128, 512]) for i in range(3)]

        consts_in = signal("consts_in", 0)
        fills = ctx.enter_context(nc.semaphore("fills"))
        setup_pool = signal("setup_pool", 0)
        setup_dve = signal("setup_dve", 0)
        loaded = [signal(f"loaded{i}", 64 if i < 3 else 96) for i in range(LOADS)]
        k_stacked = signal("k_stacked", 16 * 3 * HG * UNITS // 2)
        staged = [signal(f"staged{i}", 16 * (3 * HG + HQ)) for i in range(UNITS // 2)]
        stored = [signal(f"stored{i}", 64 if i < 3 else 96, 16) for i in range(4)]
        xT_made = signal("xT_made", UNITS)
        x_kept = signal("x_kept", UNITS)
        xh_made = signal("xh_made", UNITS)
        xl_made = signal("xl_made", UNITS)
        x_stats = signal("x_stats", UNITS)
        q_made = signal("q_made", UNITS)
        k_made = signal("k_made", UNITS)
        qh_made = signal("qh_made", UNITS)
        ql_made = signal("ql_made", UNITS)
        kh_made = signal("kh_made", UNITS)
        kl_made = signal("kl_made", UNITS)
        v_made = signal("v_made", UNITS)
        vh_made = signal("vh_made", 2 * UNITS)
        vl_made = signal("vl_made", 2 * UNITS)
        scores_made = signal("scores_made", STEPS)
        biased = signal("biased", STEPS)
        maxed = signal("maxed", STEPS)
        shifted = signal("shifted", STEPS)
        turned = signal("turned", 2 * STEPS)
        p32_made = signal("p32_made", 2 * STEPS)
        ph_made = signal("ph_made", 2 * STEPS)
        pl_made = signal("pl_made", 2 * STEPS)
        pv_made = signal("pv_made", STEPS)
        rden_made = signal("rden_made", 2 * UNITS)
        o_made = signal("o_made", 4 * UNITS)
        oT_made = signal("oT_made", UNITS)
        oh_made = signal("oh_made", UNITS)
        ol_made = signal("ol_made", UNITS)
        proj_made = signal("proj_made", UNITS)
        x1_made = signal("x1_made", UNITS)
        x1_stats = signal("x1_stats", UNITS)
        wrapped = signal("wrapped", 1)
        norm_pe = [signal("norm1_pe", 3), signal("norm2_pe", 2)]
        norm_dve = [signal("norm1_dve", 13), signal("norm2_dve", 11)]
        norm_act = [signal("norm1_act", 2), signal("norm2_act", 2)]
        y_made = signal("y_made", UNITS)
        sq_made = signal("sq_made", UNITS)
        ybox_step = signal("ybox_step", 3 * UNITS)
        qbox_step = signal("qbox_step", 5 * UNITS)
        ybox2_made = signal("ybox2_made", UNITS)
        den_made = signal("den_made", UNITS)
        num_made = signal("num_made", UNITS)
        ln_made = signal("ln_made", UNITS)
        rd0_made = signal("rd0_made", UNITS)
        ratio_step = signal("ratio_step", 4 * UNITS)
        resT_made = signal("resT_made", UNITS)
        tok_out_made = signal("tok_out_made", UNITS)

        def win_order(ap):
            return ap.rearrange("c (w i j) -> c i w j", w=UNITS, i=WIN)

        def image_rows(u, h2):
            tiles = 4 - h2
            first = WIN * u + h2 + SHIFT
            if u < UNITS - 1:
                return [(0, tiles, first)]
            return [(0, 2, first), (2, tiles - 2, first + 4 - SIDE)]

        def of_image(t, m):
            if isinstance(m, int):
                return t[m]
            return t[bass.ds(m, 1)].rearrange("n h w c -> (n h) w c")

        block = ctx.enter_context(nc.Block())

        @block.sync
        def _(sp):
            sp.dma_start(K[:, :], consts).then_inc(consts_in.sem, 16)
            sp.dma_start(WT[0:C, :], wT).then_inc(consts_in.sem, 16)
            sp.dma_start(WT[C:C + 1, :], bias_row).then_inc(consts_in.sem, 16)
            sp.dma_start(PT[0:C, :], pT).then_inc(consts_in.sem, 16)
            sp.dma_start(PT[C:C + 1, :], pb_row).then_inc(consts_in.sem, 16)

            def load(m, u):
                slot = u % LOADS
                if u >= LOADS:
                    sp.wait_ge(xT_made.sem, xT_made.at(m, u - LOADS + 1))
                elif not (isinstance(m, int) and m == 0):
                    sp.wait_ge(xT_made.sem, xT_made.at(m, u - LOADS + 1))
                for h2 in range(2):
                    for t, n, row in image_rows(u, h2):
                        src = of_image(x, m)[row:row + 2 * n - 1:2, :, :].rearrange("t w c -> w t c")
                        sp.dma_start(tok_in[slot][SIDE * h2:SIDE * h2 + SIDE, t:t + n, :], src
                                     ).then_inc(loaded[slot].sem, 16)

            def value(v):
                return v if isinstance(v, int) else sp.to_reg(v)

            def stage(m, d):
                b = d % 2
                first = isinstance(m, int) and m == 0
                k_parts, q_parts = value(kl_made.at(m, 2 * d + 2)), value(ql_made.at(m, 2 * d + 2))
                spread = value(staged[d - 1].at(m + (d > 0), 0))
                used = value(scores_made.at(m, 2 * PAIRS * (d - 1))) if d >= 2 or not first else None
                sp.wait_ge(kl_made.sem, k_parts)
                if d or not first:
                    sp.wait_ge(staged[d - 1].sem, spread)
                for r, part in enumerate((0, 0, 1)):
                    for gq in range(HG):
                        sp.dma_start(KS[r:128:4, gq, :], kn[part][b][32 * gq:32 * gq + 32, :]
                                     ).then_inc(k_stacked.sem, 16)
                sp.wait_ge(ql_made.sem, q_parts)
                if used is not None:
                    sp.wait_ge(scores_made.sem, used)
                for r, part in enumerate((0, 1, 0)):
                    for gq in range(HG):
                        sp.dma_start(QS[b][r:128:4, gq, 0:2 * TOK], qn[part][b][32 * gq:32 * gq + 32, :]
                                     ).then_inc(staged[d].sem, 16)
                sp.wait_ge(k_stacked.sem, k_stacked.at(m, 16 * 3 * HG * (d + 1)))
                for i in range(HQ):
                    rows = slice(32 * i, 32 * i + 32)
                    sp.dma_start(KE[b][rows, i::HQ, :], KS[rows, :, :]).then_inc(staged[d].sem, 16)

            def store(m, v):
                slot = v % 4
                sp.wait_ge(tok_out_made.sem, tok_out_made.at(m, v + 1))
                for h2 in range(2):
                    for t, n, row in image_rows(v, h2):
                        dst = of_image(out, m)[row:row + 2 * n - 1:2, :, :].rearrange("t w c -> w t c")
                        sp.dma_start(dst, tok_out[slot][SIDE * h2:SIDE * h2 + SIDE, t:t + n, :]
                                     ).then_inc(stored[slot].sem, 16)

            for s in range(4):
                sp.dma_start(tok_out[s][0:1, 0, :], pb_row).then_inc(stored[s].sem, 16)
            sp.wait_ge(fills, 1)
            for w in range(2):
                for q in range(L):
                    i, j = q // WIN, q % WIN
                    src = flipped[WIN - 1 - i:2 * WIN - 1 - i, WIN - 1 - j:2 * WIN - 1 - j, :]
                    sp.dma_start(bias_raw[64 * w + q:64 * w + q + 1, :, :].rearrange("p (i j) h -> p i j h", i=WIN),
                                 src.rearrange("(o i) j h -> o i j h", o=1)).then_inc(consts_in.sem, 16)

            def image(n, more):
                if more:
                    for u in range(LOADS):
                        load(n + 1, u)
                for d in range(2, UNITS // 2):
                    stage(n, d)
                    if more:
                        load(n + 1, 2 * d)
                        load(n + 1, 2 * d + 1)
                if more:
                    stage(n + 1, 0)
                for v in range(UNITS):
                    store(n, v)
                if more:
                    stage(n + 1, 1)

            for u in range(UNITS):
                load(0, u)
            stage(0, 0)
            stage(0, 1)
            with sp.Fori(0, IMAGES - 1) as n:
                image(n, True)
            image(IMAGES - 1, False)
            for s in range(4):
                sp.wait_ge(stored[s].sem, stored[s].at(IMAGES, 0))

        @block.tensor
        def _(pe):
            def turn_x(m, u, after_o):
                b = pM[2]
                slot = u % LOADS
                count = 32 * (u // LOADS + 1) + (32 if slot == 3 and u >= LOADS else 0)
                pe.wait_ge(loaded[slot].sem, loaded[slot].at(m, count))
                if after_o is not None:
                    pe.wait_ge(oh_made.sem, oh_made.at(*after_o))
                    pe.wait_ge(ol_made.sem, ol_made.at(*after_o))
                if u:
                    pe.wait_ge(xh_made.sem, xh_made.at(m, u))
                for t in range(4):
                    k = 2 * SIDE if t < 3 else SIDE
                    mm = pe.transpose(b[0:C, 2 * SIDE * t:2 * SIDE * t + k], tok_in[slot][0:k, t, :],
                                      roll[0:k, 0:k])
                mm.then_inc(xT_made.sem, 1)

            def project(dst, col, u, done):
                xs = slice(TOK * u, TOK * u + TOK)
                pe.matmul(dst[0:C, 0:TOK], WH[:, col:col + C], XH[:, xs], start=True, stop=False)
                pe.matmul(dst[0:C, 0:TOK], WH[:, col:col + C], XL[:, xs], start=False, stop=False)
                pe.matmul(dst[0:C, 0:TOK], WL[:, col:col + C], XH[:, xs], start=False, stop=True
                          ).then_inc(done.sem, 1)

            def qk(m, u):
                if u == 0:
                    pe.wait_ge(norm_dve[0].sem, norm_dve[0].at(m, 13))
                    pe.wait_ge(xl_made.sem, xl_made.at(m, UNITS))
                if u >= 6:
                    pe.wait_ge(x1_made.sem, x1_made.at(m, u - 5))
                elif u >= 1:
                    pe.wait_ge(ql_made.sem, ql_made.at(m, u))
                project(pM[0], 0, u, q_made)
                if u >= 4:
                    pe.wait_ge(vl_made.sem, vl_made.at(m, 2 * (u - 3)))
                elif u >= 1:
                    pe.wait_ge(kl_made.sem, kl_made.at(m, u))
                project(pM[1], C, u, k_made)

            def values(m, u):
                if u + 4 <= UNITS:
                    pe.wait_ge(kl_made.sem, kl_made.at(m, u + 4))
                else:
                    pe.wait_ge(vl_made.sem, vl_made.at(m, 2 * u))
                for w in range(2):
                    for p in range(PAIRS):
                        at = TOK * u + L * (2 * p + w)
                        xh, xl = XH[:, at:at + 64], XL[:, at:at + 64]
                        col = (PAIRS * w + p) * C // 2
                        for part, (lhs, rhs) in enumerate(((xh, WH), (xh, WL), (xl, WH))):
                            for h in range(2):
                                wv = rhs[:, 2 * C:3 * C].rearrange("c (a h d) -> c a h d", h=2, d=D)
                                mm = pe.matmul(pM[1][64 * h:64 * h + 64, col:col + C // 2], lhs, wv[:, :, h, :],
                                               start=(part == 0), stop=(part == 2))
                mm.then_inc(v_made.sem, 1)

            def scores(m, j):
                u, p = divmod(j, PAIRS)
                if j % (2 * PAIRS) == 0:
                    pe.wait_ge(staged[u // 2].sem, staged[u // 2].at(m + 1, 0))
                if j:
                    pe.wait_ge(biased.sem, biased.at(m, j))
                Q, E = QS[u // 2 % 2], KE[u // 2 % 2]
                for w in range(2):
                    at = TOK * (u % 2) + L * (2 * p + w)
                    for gq, h0, h1 in ((0, 0, 4), (1, 4, 6), (1, 6, 8), (2, 8, 12)):
                        bank, col = divmod(h0 * L, HALF)
                        mm = pe.matmul(pS[64 * w:64 * w + 64, bank, col:col + (h1 - h0) * L],
                                       Q[:, gq, at:at + 64], E[:, h0:h1, at:at + L], start=True, stop=True)
                mm.then_inc(scores_made.sem, 1)

            def turn_scores(m, j):
                pe.wait_ge(shifted.sem, shifted.at(m, j + 1))
                for c in range(2):
                    if j:
                        pe.wait_ge(ph_made.sem, ph_made.at(m, 2 * j - 1 + c))
                    for h in range(3):
                        h0 = 2 * (3 * c + h)
                        mm = pe.transpose(pP[:, c, 128 * h:128 * h + 128], T[j % 2][:, h0:h0 + 2, :], ident)
                    mm.then_inc(turned.sem, 1)

            def times_v(m, j):
                u, p = divmod(j, PAIRS)
                pe.wait_ge(pl_made.sem, pl_made.at(m, 2 * j + 2))
                if p == 0:
                    pe.wait_ge(vl_made.sem, vl_made.at(m, 2 * u + 2))
                if p % 2 == 0 and j:
                    pe.wait_ge(o_made.sem, o_made.at(m, j))
                for h in range(HP):
                    dst = pO[:, VC * (HP * (p % 2) + h):VC * (HP * (p % 2) + h + 1)]
                    pr_h = PRH[j % 4][:, 2 * h:2 * h + 2, :]
                    pr_l = PRL[j % 4][:, 2 * h:2 * h + 2, :]
                    v_h = VH[u % 2][:, HP * p + h, :, :, :]
                    v_l = VL[u % 2][:, HP * p + h, :, :, :]
                    pe.matmul(dst, pr_h, v_h, start=True, stop=False)
                    pe.matmul(dst, pr_h, v_l, start=False, stop=False)
                    mm = pe.matmul(dst, pr_l, v_h, start=False, stop=True)
                mm.then_inc(pv_made.sem, 1)

            def turn_o(m, u, x_read):
                pe.wait_ge(o_made.sem, o_made.at(m, 4 * u + 4))
                if x_read is not None:
                    pe.wait_ge(xh_made.sem, xh_made.at(*x_read))
                elif u:
                    pe.wait_ge(ol_made.sem, ol_made.at(m, u))
                for p in range(PAIRS):
                    mm = pe.transpose(pM[2][0:C, 128 * p:128 * p + 128], O[u % 2][:, p, :], ident)
                mm.then_inc(oT_made.sem, 1)

            def project_o(m, u):
                pe.wait_ge(oh_made.sem, oh_made.at(m, u + 1))
                pe.wait_ge(ol_made.sem, ol_made.at(m, u + 1))
                if u + 5 < UNITS:
                    pe.wait_ge(ql_made.sem, ql_made.at(m, u + 6))
                else:
                    pe.wait_ge(x1_made.sem, x1_made.at(m, u))
                dst = pM[0][0:C, 0:TOK]
                pe.matmul(dst, PH[:, :], OH[:, :], start=True, stop=False)
                pe.matmul(dst, PH[:, :], OL[:, :], start=False, stop=False)
                pe.matmul(dst, PL[:, :], OH[:, :], start=False, stop=True).then_inc(proj_made.sem, 1)

            def norm_sums(m, which, bank):
                s = norm_dve[which]
                pe.wait_ge(s.sem, s.at(m, 1))
                pe.matmul(bank[0:C, 0:1], group, mv[which][:, 0:1], start=True, stop=True
                          ).then_inc(norm_pe[which].sem, 1)
                pe.wait_ge(s.sem, s.at(m, 3))
                pe.matmul(bank[0:C, 1:2], group, g[which][:, V2:V2 + 1], start=True, stop=True
                          ).then_inc(norm_pe[which].sem, 1)

            def norm_bias(m):
                pe.wait_ge(norm_dve[0].sem, norm_dve[0].at(m, 9))
                pe.matmul(pM[1][C:C + 1, 2:2 + 3 * C], g[0][:, NB:NB + 1], WT[0:C, :], start=True, stop=True
                          ).then_inc(norm_pe[0].sem, 1)

            def band_sums(m, v):
                pe.wait_ge(qbox_step.sem, qbox_step.at(m, 5 * v + 5))
                if v:
                    pe.wait_ge(ratio_step.sem, ratio_step.at(m, 4 * v - 2))
                pe.matmul(pP[0:C, 0, 0:TOK], band, qbox[v % 2][:, :, :], start=True, stop=True
                          ).then_inc(den_made.sem, 1)
                pe.wait_ge(ybox2_made.sem, ybox2_made.at(m, v + 1))
                pe.matmul(pP[0:C, 1, 0:TOK], band, ybox2[v % 2][:, :, :], start=True, stop=True
                          ).then_inc(num_made.sem, 1)

            def turn_result(m, v):
                pe.wait_ge(ratio_step.sem, ratio_step.at(m, 4 * v + 4))
                if v:
                    pe.wait_ge(tok_out_made.sem, tok_out_made.at(m, v))
                for t in range(4):
                    mm = pe.transpose(pO[0:2 * SIDE, C * t:C * t + C],
                                      res[v % 2][:, 2 * SIDE * t:2 * SIDE * t + 2 * SIDE], ident[0:C, 0:C])
                mm.then_inc(resT_made.sem, 1)

            def image(n, more):
                for j in range(STEPS):
                    u, p = divmod(j, PAIRS)
                    if j + 1 < STEPS:
                        scores(n, j + 1)
                    if p == 0 and u + 4 < UNITS:
                        qk(n, u + 4)
                    if p == 1 and u >= 2 and more:
                        turn_x(n + 1, u - 2, (n, u - 1))
                    turn_scores(n, j)
                    if p == 2 and u + 1 < UNITS:
                        values(n, u + 1)
                    if p == 3 and u >= 1:
                        project_o(n, u - 1)
                    if j >= 2:
                        times_v(n, j - 2)
                    if p == 2 and u >= 1:
                        turn_o(n, u - 1, (n + 1, u - 1) if more and u >= 2 else None)
                times_v(n, STEPS - 2)
                times_v(n, STEPS - 1)
                if more:
                    turn_x(n + 1, UNITS - 2, (n, UNITS - 1))
                turn_o(n, UNITS - 1, (n + 1, UNITS - 1) if more else None)
                project_o(n, UNITS - 1)
                if more:
                    turn_x(n + 1, UNITS - 1, (n, UNITS))
                norm_sums(n, 1, pO)
                if more:
                    norm_sums(n + 1, 0, pM[1])
                    norm_bias(n + 1)
                    qk(n + 1, 0)
                    qk(n + 1, 1)
                band_sums(n, 0)
                for v in range(1, UNITS):
                    band_sums(n, v)
                    turn_result(n, v - 1)
                    if more and v in (2, 3):
                        qk(n + 1, v)
                    if more and v == 4:
                        values(n + 1, 0)
                    if more and v == 5:
                        scores(n + 1, 0)
                turn_result(n, UNITS - 1)

            pe.wait_ge(setup_dve.sem, 1)
            for u in range(UNITS):
                turn_x(0, u, None)
            norm_sums(0, 0, pM[1])
            norm_bias(0)
            for u in range(4):
                qk(0, u)
            values(0, 0)
            scores(0, 0)
            with pe.Fori(0, IMAGES - 1) as n:
                image(n, True)
            image(IMAGES - 1, False)

        @block.scalar
        def _(act):
            act.preload_act_table_set("natural_log_exp_and_others")

            def keep_x(m, u, x1_done):
                act.wait_ge(xT_made.sem, xT_made.at(m, u + 1))
                if x1_done is not None:
                    act.wait_ge(x1_made.sem, x1_made.at(*x1_done))
                src = pM[2][0:C, 0:TOK].rearrange("c (i w j) -> c i w j", i=WIN, w=UNITS)
                act.activation(win_order(X[:, TOK * u:TOK * u + TOK]), src, ACT.Copy).then_inc(x_kept.sem, 1)
                act.activation(win_order(XH[0:C, TOK * u:TOK * u + TOK]), src, ACT.Copy
                               ).then_inc(xh_made.sem, 1)

            def high_qk(m, u):
                act.wait_ge(q_made.sem, q_made.at(m, u + 1))
                last, b, s = u // 2 - 2, u // 2 % 2, slice(TOK * (u % 2), TOK * (u % 2) + TOK)
                if last >= 0 or not (isinstance(m, int) and m == 0):
                    act.wait_ge(staged[last].sem, staged[last].at(m + 1 if last >= 0 else m, 0))
                act.activation(qn[0][b][:, s], pM[0][0:C, 0:TOK], ACT.Copy).then_inc(qh_made.sem, 1)
                act.wait_ge(k_made.sem, k_made.at(m, u + 1))
                act.activation(kn[0][b][:, s], pM[1][0:C, 0:TOK], ACT.Copy).then_inc(kh_made.sem, 1)

            def high_v(m, u):
                act.wait_ge(v_made.sem, v_made.at(m, u + 1))
                if u >= 2:
                    act.wait_ge(pv_made.sem, pv_made.at(m, PAIRS * (u - 1)))
                for h in range(2):
                    ps = slice(64 * h, 64 * h + L)
                    act.activation(VH[u % 2][ps, :, :, h, 0:D].rearrange("p a w d -> p w a d"),
                                   pM[1][ps, 0:PAIRS * C].rearrange("p (w a d) -> p w a d", w=2, d=D), ACT.Copy
                                   ).then_inc(vh_made.sem, 1)

            def exponentials(m, j):
                for c in range(2):
                    act.wait_ge(turned.sem, turned.at(m, 2 * j + c + 1))
                    if j >= 2:
                        act.wait_ge(pl_made.sem, pl_made.at(m, 2 * (j - 2) + c + 1))
                    src = pP[:, c, 0:6 * 64].rearrange("p (a q) -> p a q", q=64)[:, :, 0:L]
                    act.activation(P32[j % 2][:, 6 * c:6 * c + 6, :], src, ACT.Exp).then_inc(p32_made.sem, 1)
                    if j >= 4:
                        act.wait_ge(pv_made.sem, pv_made.at(m, j - 3))
                    act.activation(PRH[j % 4][:, 6 * c:6 * c + 6, 0:L], src, ACT.Exp).then_inc(ph_made.sem, 1)

            def high_o(m, u):
                act.wait_ge(oT_made.sem, oT_made.at(m, u + 1))
                if u:
                    act.wait_ge(proj_made.sem, proj_made.at(m, u))
                src = pM[2][0:C, :].rearrange("c (a q) -> c a q", q=64)[:, :, 0:L]
                act.activation(OH[0:C, :].rearrange("c (a q) -> c a q", q=L), src, ACT.Copy
                               ).then_inc(oh_made.sem, 1)

            def norm_root(m, which):
                gw = g[which]
                s = norm_act[which]
                act.wait_ge(norm_dve[which].sem, norm_dve[which].at(m, 4))
                act.activation(gw[:, LN:LN + 1], gw[:, VE:VE + 1], ACT.Ln).then_inc(s.sem, 1)
                act.wait_ge(s.sem, s.at(m, 1))
                act.activation(gw[:, R0:R0 + 1], gw[:, LN:LN + 1], ACT.Exp, scale=-0.5).then_inc(s.sem, 1)

            def normalise(m, v):
                if v == 0:
                    act.wait_ge(norm_dve[1].sem, norm_dve[1].at(m, 11))
                    act.wait_ge(wrapped.sem, wrapped.at(m, 1))
                rows = slice(WIN * v, WIN * v + WIN)
                cols = slice(LEFT, LEFT + SIDE)
                if v >= 2:
                    act.wait_ge(ybox_step.sem, ybox_step.at(m, 3 * (v - 1)))
                act.activation(Y[v % 2][:, :, cols], X1[:, rows, cols], ACT.Identity,
                               bias=g[1][:, NB:NB + 1], scale=g[1][:, RS:RS + 1]).then_inc(y_made.sem, 1)
                if v >= 2:
                    act.wait_ge(qbox_step.sem, qbox_step.at(m, 5 * (v - 2) + 3))
                act.activation(SQ[v % 2][:, :, cols], X1[:, rows, cols], ACT.Square,
                               bias=g[1][:, NB5:NB5 + 1], scale=g[1][:, RS5:RS5 + 1]).then_inc(sq_made.sem, 1)

            def square_box(m, v):
                act.wait_ge(ybox_step.sem, ybox_step.at(m, 3 * v + 3))
                if v >= 2:
                    act.wait_ge(num_made.sem, num_made.at(m, v - 1))
                act.activation(ybox2[v % 2][:, :, :], ybox[v % 2][:, :, :], ACT.Square
                               ).then_inc(ybox2_made.sem, 1)

            def invert(m, v):
                act.wait_ge(den_made.sem, den_made.at(m, v + 1))
                if v:
                    act.wait_ge(rd0_made.sem, rd0_made.at(m, v))
                act.activation(lnd[:, :], pP[0:C, 0, 0:TOK], ACT.Ln, bias=tiny[:, 0:1]).then_inc(ln_made.sem, 1)
                act.wait_ge(ln_made.sem, ln_made.at(m, v + 1))
                if v >= 2:
                    act.wait_ge(ratio_step.sem, ratio_step.at(m, 4 * (v - 2) + 2))
                act.activation(rd0[v % 2][:, :], lnd[:, :], ACT.Exp, scale=-1.0).then_inc(rd0_made.sem, 1)

            def keep_result(m, v):
                act.wait_ge(resT_made.sem, resT_made.at(m, v + 1))
                slot = v % 4
                if v >= 4:
                    act.wait_ge(stored[slot].sem, stored[slot].at(m, 32))
                else:
                    act.wait_ge(stored[slot].sem, stored[slot].at(m, 0))
                act.activation(tok_out[slot][:, :, :].rearrange("p t c -> p (t c)"),
                               pO[0:2 * SIDE, 0:4 * C], ACT.Copy).then_inc(tok_out_made.sem, 1)

            def image(n, more):
                for j in range(STEPS):
                    u, p = divmod(j, PAIRS)
                    if p == 0 and u + 4 < UNITS:
                        high_qk(n, u + 4)
                    exponentials(n, j)
                    if p == 1 and u >= 2 and more:
                        keep_x(n + 1, u - 2, (n, u - 1))
                    if p == 2 and u + 1 < UNITS:
                        high_v(n, u + 1)
                    if p == 2 and u >= 1:
                        high_o(n, u - 1)
                if more:
                    keep_x(n + 1, UNITS - 2, (n, UNITS - 1))
                high_o(n, UNITS - 1)
                if more:
                    keep_x(n + 1, UNITS - 1, (n, UNITS))
                norm_root(n, 1)
                if more:
                    norm_root(n + 1, 0)
                normalise(n, 0)
                if more:
                    high_qk(n + 1, 0)
                    high_qk(n + 1, 1)
                normalise(n, 1)
                for v in range(UNITS):
                    square_box(n, v)
                    if v in (2, 3) and more:
                        high_qk(n + 1, v)
                    invert(n, v)
                    if v + 2 < UNITS:
                        normalise(n, v + 2)
                    if v:
                        keep_result(n, v - 1)
                    if v == 4 and more:
                        high_v(n + 1, 0)
                keep_result(n, UNITS - 1)

            act.wait_ge(setup_pool.sem, 1)
            for u in range(UNITS):
                keep_x(0, u, None)
            norm_root(0, 0)
            for u in range(4):
                high_qk(0, u)
            high_v(0, 0)
            with act.Fori(0, IMAGES - 1) as n:
                image(n, True)
            image(IMAGES - 1, False)

        @block.vector
        def _(dve):
            def add_bias(m, j):
                u, p = divmod(j, PAIRS)
                dve.wait_ge(scores_made.sem, scores_made.at(m, j + 1))
                if j >= 2:
                    dve.wait_ge(turned.sem, turned.at(m, 2 * (j - 1)))
                tab = table[2 * (u == UNITS - 1) + (p == PAIRS - 1)]
                dve.tensor_tensor(T[j % 2][:, :, 0:L].rearrange("p (b h) k -> p b h k", b=2),
                                  pS[:, :, 0:HALF].rearrange("p b (h k) -> p b h k", k=L),
                                  tab[:, :].rearrange("p (b h k) -> p b h k", b=2, k=L), ALU.add
                                  ).then_inc(biased.sem, 1)
                dve.wait_ge(biased.sem, biased.at(m, j + 1))
                dve.tensor_reduce(MX[j % 2][:, :], T[j % 2][:, :, 0:L],
                                  AX.X, ALU.max).then_inc(maxed.sem, 1)

            def low_qk(m, u):
                dve.wait_ge(qh_made.sem, qh_made.at(m, u + 1))
                b, s = u // 2 % 2, slice(TOK * (u % 2), TOK * (u % 2) + TOK)
                dve.tensor_tensor(qn[1][b][:, s], pM[0][0:C, 0:TOK], qn[0][b][:, s], ALU.subtract
                                  ).then_inc(ql_made.sem, 1)
                dve.wait_ge(kh_made.sem, kh_made.at(m, u + 1))
                dve.tensor_tensor(kn[1][b][:, s], pM[1][0:C, 0:TOK], kn[0][b][:, s], ALU.subtract
                                  ).then_inc(kl_made.sem, 1)

            def low_v(m, u):
                for h in range(2):
                    ps = slice(64 * h, 64 * h + L)
                    dve.wait_ge(vh_made.sem, vh_made.at(m, 2 * u + h + 1))
                    dve.tensor_tensor(VL[u % 2][ps, :, :, h, 0:D].rearrange("p a w d -> p w a d"),
                                      pM[1][ps, 0:PAIRS * C].rearrange("p (w a d) -> p w a d", w=2, d=D),
                                      VH[u % 2][ps, :, :, h, 0:D].rearrange("p a w d -> p w a d"), ALU.subtract
                                      ).then_inc(vl_made.sem, 1)

            def divide_o(m, u, half):
                dve.wait_ge(pv_made.sem, pv_made.at(m, PAIRS * u + 2 * half + 2))
                got = pO[:, 0:2 * HP * VC].rearrange("p (a w h d) -> p a w h d", w=2, h=2, d=D + 1)
                if u or half:
                    dve.wait_ge(o_made.sem, o_made.at(m, 4 * u + 2 * half))
                dve.reciprocal(rden[:, :, :, :], got[:, :, :, :, D]).then_inc(rden_made.sem, 1)
                dve.wait_ge(rden_made.sem, rden_made.at(m, 2 * u + half + 1))
                if u >= 2:
                    dve.wait_ge(oT_made.sem, oT_made.at(m, u - 1))
                for w in range(2):
                    ps = slice(64 * w, 64 * w + 64)
                    dst = O[u % 2][ps, 2 * half:2 * half + 2, :].rearrange("p a (b h d) -> p (a b) h d", h=2, d=D)
                    by = rden[ps, :, w, :].unsqueeze(3).broadcast_to([64, 2 * HP, 2, D])
                    dve.tensor_tensor(dst, got[ps, :, w, :, 0:D], by, ALU.mult).then_inc(o_made.sem, 1)

            def low_o(m, u):
                dve.wait_ge(oh_made.sem, oh_made.at(m, u + 1))
                src = pM[2][0:C, :].rearrange("c (a q) -> c a q", q=64)[:, :, 0:L]
                dve.tensor_tensor(OL[0:C, :].rearrange("c (a q) -> c a q", q=L), src,
                                  OH[0:C, :].rearrange("c (a q) -> c a q", q=L), ALU.subtract
                                  ).then_inc(ol_made.sem, 1)

            def add_x(m, u):
                dve.wait_ge(proj_made.sem, proj_made.at(m, u + 1))

                def by_row(ap):
                    return ap.rearrange("c (w i j) -> c w i j", w=UNITS, i=WIN)

                at = LEFT + SHIFT
                dst = X1[:, WIN * u:WIN * u + WIN, at:at + SIDE].rearrange("c i (w j) -> c w i j", j=WIN)
                dve.tensor_tensor(dst, by_row(pM[0][0:C, 0:TOK]), by_row(X[:, TOK * u:TOK * u + TOK]), ALU.add
                                  ).then_inc(x1_made.sem, 1)
                dve.wait_ge(x1_made.sem, x1_made.at(m, u + 1))
                dve.bn_stats(stats[1][:, u, :], X1[:, WIN * u:WIN * u + WIN, at:at + SIDE]
                             ).then_inc(x1_stats.sem, 1)

            def stats_of_x(m, u):
                dve.wait_ge(x_kept.sem, x_kept.at(m, u + 1))
                dve.bn_stats(stats[0][:, u, :], X[:, TOK * u:TOK * u + TOK]).then_inc(x_stats.sem, 1)

            def norm(m, which, bank):
                gw, mw, s = g[which], mv[which], norm_dve[which]
                count = [0]

                def col(i):
                    return gw[:, i:i + 1]

                def link(ins):
                    count[0] += 1
                    ins.then_inc(s.sem, 1)
                    dve.wait_ge(s.sem, s.at(m, count[0]))

                dve.wait_ge((x_stats, x1_stats)[which].sem, (x_stats, x1_stats)[which].at(m, UNITS))
                dve.memset(col(GATE), 0.0)
                link(dve.bn_aggr(mw[:, :], stats[which][:, :, :].rearrange("c u s -> c (u s)")))
                dve.wait_ge(norm_pe[which].sem, norm_pe[which].at(m, 1))
                link(dve.tensor_tensor(col(DEV), mw[:, 0:1], bank[0:C, 0:1], ALU.subtract))
                link(dve.scalar_tensor_tensor(out=col(V2), in0=col(DEV), scalar=col(DEV), in1=mw[:, 1:2],
                                              op0=ALU.mult, op1=ALU.add))
                dve.wait_ge(norm_pe[which].sem, norm_pe[which].at(m, 2))
                link(dve.tensor_scalar(col(VE), bank[0:C, 1:2], EPS, None, ALU.add))
                dve.wait_ge(norm_act[which].sem, norm_act[which].at(m, 2))
                link(dve.tensor_tensor(col(SQR), col(R0), col(R0), ALU.mult))
                link(dve.tensor_tensor(col(SQV), col(SQR), col(VE), ALU.mult))
                link(dve.tensor_scalar(col(NW), col(SQV), -0.5, 1.5, ALU.mult, ALU.add))
                link(dve.tensor_tensor(col(RS), col(R0), col(NW), ALU.mult))
                link(dve.scalar_tensor_tensor(out=col(NB), in0=bank[0:C, 0:1], scalar=-1.0, in1=col(RS),
                                              op0=ALU.mult, op1=ALU.mult))
                if which == 0:
                    link(dve.tensor_scalar(W32[0:C, :], WT[0:C, :], col(RS), None, ALU.mult))
                    dve.wait_ge(norm_pe[0].sem, norm_pe[0].at(m, 3))
                    link(dve.tensor_tensor(W32[C:C + 1, :], bank[C:C + 1, 2:2 + 3 * C], WT[C:C + 1, :], ALU.add))
                    link(dve.tensor_copy(WH[:, :], W32[:, :]))
                    link(dve.tensor_tensor(WL[:, :], W32[:, :], WH[:, :], ALU.subtract))
                else:
                    link(dve.tensor_scalar(col(RS5), col(RS), 5.0 ** 0.5, None, ALU.mult))
                    link(dve.tensor_scalar(col(NB5), col(NB), 5.0 ** 0.5, None, ALU.mult))

            def wrap(m):
                at = LEFT + SIDE
                dve.wait_ge(x1_made.sem, x1_made.at(m, UNITS))
                dve.tensor_copy(X1[:, :, LEFT:LEFT + SHIFT], X1[:, :, at:at + SHIFT]).then_inc(wrapped.sem, 1)

            def box_of_squares(m, v):
                s = SQ[v % 2]
                q = qbox[v % 2]
                k = 5 * v
                dve.wait_ge(sq_made.sem, sq_made.at(m, v + 1))
                dve.tensor_tensor(q2[:, :, 0:59], s[:, :, 0:59], s[:, :, 1:60], ALU.add).then_inc(qbox_step.sem, 1)
                dve.wait_ge(qbox_step.sem, qbox_step.at(m, k + 1))
                dve.tensor_tensor(q4[:, :, 0:56], q2[:, :, 0:56], q2[:, :, 2:58], ALU.add
                                  ).then_inc(qbox_step.sem, 1)
                if v >= 2:
                    dve.wait_ge(den_made.sem, den_made.at(m, v - 1))
                dve.wait_ge(qbox_step.sem, qbox_step.at(m, k + 2))
                dve.tensor_tensor(q[:, :, :], q4[:, :, 0:56], s[:, :, 4:60], ALU.add).then_inc(qbox_step.sem, 1)
                dve.wait_ge(qbox_step.sem, qbox_step.at(m, k + 3))
                dve.tensor_scalar(q[:, :, 0:56:55], q[:, :, 0:56:55], 0.6, None, ALU.mult
                                  ).then_inc(qbox_step.sem, 1)
                dve.tensor_scalar(q[:, :, 1:55:53], q[:, :, 1:55:53], 0.8, None, ALU.mult
                                  ).then_inc(qbox_step.sem, 1)

            def ratio(m, v):
                k = 4 * v
                s = ratio_step
                dve.wait_ge(rd0_made.sem, rd0_made.at(m, v + 1))
                if v:
                    dve.wait_ge(s.sem, s.at(m, k - 1))
                dve.scalar_tensor_tensor(out=de[:, :], in0=pP[0:C, 0, 0:TOK], scalar=TINY, in1=rd0[v % 2][:, :],
                                         op0=ALU.add, op1=ALU.mult).then_inc(s.sem, 1)
                dve.wait_ge(num_made.sem, num_made.at(m, v + 1))
                dve.scalar_tensor_tensor(out=nu[:, :], in0=pP[0:C, 1, 0:TOK], scalar=TINY, in1=rd0[v % 2][:, :],
                                         op0=ALU.add, op1=ALU.mult).then_inc(s.sem, 1)
                dve.wait_ge(s.sem, s.at(m, k + 2))
                dve.scalar_tensor_tensor(out=ra[:, :], in0=de[:, :], scalar=-2.0, in1=nu[:, :],
                                         op0=ALU.add, op1=ALU.mult).then_inc(s.sem, 1)
                dve.wait_ge(s.sem, s.at(m, k + 3))
                if v >= 2:
                    dve.wait_ge(resT_made.sem, resT_made.at(m, v - 1))
                dve.tensor_tensor(res[v % 2][:, 0:TOK].rearrange("c (i w) -> c i w", i=WIN),
                                  X1[:, WIN * v:WIN * v + WIN, LEFT:LEFT + SIDE],
                                  ra[:, :].rearrange("c (i w) -> c i w", i=WIN), ALU.subtract
                                  ).then_inc(s.sem, 1)

            def image(n, more):
                for j in range(STEPS):
                    u, p = divmod(j, PAIRS)
                    if p == 0 and u >= 2:
                        add_x(n, u - 2)
                    if p == 0 and u >= 1:
                        divide_o(n, u - 1, 0)
                    if p == 2 and u >= 1:
                        divide_o(n, u - 1, 1)
                    if j + 1 < STEPS:
                        add_bias(n, j + 1)
                    if p == 0 and u + 4 < UNITS:
                        low_qk(n, u + 4)
                    if p == 2 and u >= 2 and more:
                        stats_of_x(n + 1, u - 2)
                    if p == 2 and u + 1 < UNITS:
                        low_v(n, u + 1)
                    if p == 3 and u >= 1:
                        low_o(n, u - 1)
                divide_o(n, UNITS - 1, 0)
                add_x(n, UNITS - 2)
                divide_o(n, UNITS - 1, 1)
                if more:
                    stats_of_x(n + 1, UNITS - 2)
                low_o(n, UNITS - 1)
                add_x(n, UNITS - 1)
                wrap(n)
                norm(n, 1, pO)
                if more:
                    stats_of_x(n + 1, UNITS - 1)
                    norm(n + 1, 0, pM[1])
                box_of_squares(n, 0)
                if more:
                    low_qk(n + 1, 0)
                    low_qk(n + 1, 1)
                for v in range(UNITS):
                    if v + 1 < UNITS:
                        box_of_squares(n, v + 1)
                    ratio(n, v)
                    if v in (2, 3) and more:
                        low_qk(n + 1, v)
                    if v == 4 and more:
                        low_v(n + 1, 0)
                    if v == 6 and more:
                        add_bias(n + 1, 0)

            dve.wait_ge(consts_in.sem, 16 * (5 + 2 * L))
            dve.wait_ge(setup_pool.sem, 1)
            done = [0]
            own = ctx.enter_context(nc.semaphore("setup_chain"))

            def link(ins):
                done[0] += 1
                ins.then_inc(own, 1)
                dve.wait_ge(own, done[0])

            link(dve.tensor_copy(table[0][:, :].rearrange("p (h k) -> p h k", h=HEADS),
                                 bias_raw[:, :, :].rearrange("p k h -> p h k")))
            for t in (3, 2, 1, 0):
                mask = K[:, K_MASK + L * t:K_MASK + L * t + L].unsqueeze(1).broadcast_to([128, HEADS, L])
                link(dve.tensor_tensor(table[t][:, :].rearrange("p (h k) -> p h k", h=HEADS),
                                       table[0][:, :].rearrange("p (h k) -> p h k", h=HEADS), mask, ALU.add))
            link(dve.tensor_scalar(WT[:, 0:C], WT[:, 0:C], float(D) ** -0.5, None, ALU.mult))
            link(dve.tensor_copy(PH[:, :], PT[:, :]))
            link(dve.tensor_tensor(PL[:, :], PT[:, :], PH[:, :], ALU.subtract))
            for b in range(2):
                for w in range(2):
                    link(dve.tensor_copy(VH[b][:, :, w, :, D],
                                         half_of.unsqueeze(1).broadcast_to([128, PAIRS * HP, 2])))
            dve.memset(tiny[:, :], TINY).then_inc(setup_dve.sem, 1)

            for u in range(UNITS):
                stats_of_x(0, u)
            norm(0, 0, pM[1])
            for u in range(4):
                low_qk(0, u)
            low_v(0, 0)
            add_bias(0, 0)
            with dve.Fori(0, IMAGES - 1) as n:
                image(n, True)
            image(IMAGES - 1, False)

        @block.gpsimd
        def _(pool):
            def low_x(m, u):
                pool.wait_ge(xh_made.sem, xh_made.at(m, u + 1))
                s = slice(TOK * u, TOK * u + TOK)
                pool.tensor_tensor(XL[0:C, s], X[:, s], XH[0:C, s], ALU.subtract).then_inc(xl_made.sem, 1)

            def shift(m, j):
                pool.wait_ge(maxed.sem, maxed.at(m, j + 1))
                t = T[j % 2][:, :, 0:L]
                pool.tensor_tensor(t, t, MX[j % 2][:, :].unsqueeze(2).broadcast_to([128, HEADS, L]),
                                   ALU.subtract).then_inc(shifted.sem, 1)

            def low_p(m, j):
                for c in range(2):
                    pool.wait_ge(ph_made.sem, ph_made.at(m, 2 * j + c + 1))
                    hs = slice(6 * c, 6 * c + 6)
                    pool.tensor_tensor(PRL[j % 4][:, hs, 0:L], P32[j % 2][:, hs, :], PRH[j % 4][:, hs, 0:L],
                                       ALU.subtract).then_inc(pl_made.sem, 1)

            def box(m, v):
                y = Y[v % 2]
                pool.wait_ge(y_made.sem, y_made.at(m, v + 1))
                pool.tensor_tensor(y2[:, :, 0:59], y[:, :, 0:59], y[:, :, 1:60], ALU.add).then_inc(ybox_step.sem, 1)
                pool.wait_ge(ybox_step.sem, ybox_step.at(m, 3 * v + 1))
                pool.tensor_tensor(y4[:, :, 0:56], y2[:, :, 0:56], y2[:, :, 2:58], ALU.add
                                   ).then_inc(ybox_step.sem, 1)
                if v >= 2:
                    pool.wait_ge(ybox2_made.sem, ybox2_made.at(m, v - 1))
                pool.wait_ge(ybox_step.sem, ybox_step.at(m, 3 * v + 2))
                pool.tensor_tensor(ybox[v % 2][:, :, :], y4[:, :, 0:56], y[:, :, 4:60], ALU.add
                                   ).then_inc(ybox_step.sem, 1)

            def image(n, more):
                for j in range(STEPS):
                    u, p = divmod(j, PAIRS)
                    if j:
                        low_p(n, j - 1)
                    if j + 1 < STEPS:
                        shift(n, j + 1)
                    if p == 2 and u >= 2 and more:
                        low_x(n + 1, u - 2)
                low_p(n, STEPS - 1)
                if more:
                    low_x(n + 1, UNITS - 2)
                    low_x(n + 1, UNITS - 1)
                for v in range(UNITS):
                    box(n, v)
                if more:
                    shift(n + 1, 0)

            zero = [bias_raw, XL, Y[0], Y[1], SQ[0], SQ[1], T[0], T[1], VL[0], VL[1], QS[0], QS[1], KS, KE[0], KE[1],
                    PRL[0], PRL[1], PRL[2], PRL[3], VH[0], VH[1], OL, O[0], O[1], res[0], res[1], X1]
            one = [XH, OH, PRH[0], PRH[1], PRH[2], PRH[3]]
            for t in zero:
                pool.memset(t[tuple([slice(None)] * len(t.shape))], 0.0).then_inc(fills, 1)
            for t in one:
                pool.memset(t[tuple([slice(None)] * len(t.shape))], 1.0).then_inc(fills, 1)
            pool.wait_ge(fills, len(zero) + len(one))
            pool.memset(XH[0:C, UNITS * TOK:], 0.0).then_inc(setup_pool.sem, 1)

            for u in range(UNITS):
                low_x(0, u)
            shift(0, 0)
            with pool.Fori(0, IMAGES - 1) as n:
                image(n, True)
            image(IMAGES - 1, False)


def kernel(x, L0_conv_qkv_w, L0_conv_qkv_b, L0_conv_proj_w, L0_conv_proj_b, L0_conv_rel_table):
    import concourse.bacc as bacc
    from concourse.bass_utils import run_bass_kernel_spmd

    side = 2 * WIN - 1
    arrays = {
        "x": np.ascontiguousarray(x),
        "wT": np.ascontiguousarray(np.asarray(L0_conv_qkv_w).T),
        "bias_row": np.ascontiguousarray(np.asarray(L0_conv_qkv_b).reshape(1, 3 * C)),
        "pT": np.ascontiguousarray(np.asarray(L0_conv_proj_w).T),
        "pb_row": np.ascontiguousarray(np.asarray(L0_conv_proj_b).reshape(1, C)),
        "flipped": np.ascontiguousarray(np.asarray(L0_conv_rel_table).reshape(side, side, HEADS)[::-1, ::-1]),
        "consts": shape_constants(),
    }
    nc = bacc.Bacc("TRN2", target_bir_lowering=False, num_devices=1)
    args = [nc.dram_tensor(k, a.shape, mybir.dt.from_np(a.dtype), kind="ExternalInput").ap()
            for k, a in arrays.items()]
    out = nc.dram_tensor("out", (IMAGES, SIDE, SIDE, C), F32, kind="ExternalOutput").ap()
    build(nc, *args, out)
    r = run_bass_kernel_spmd(nc, [arrays], core_ids=[0])
    return r.results[0]["out"]
```

```python
from contextlib import ExitStack

import numpy as np

import concourse.bass as bass
from concourse import mybir

F32 = mybir.dt.float32
BF16 = mybir.dt.bfloat16
ALU = mybir.AluOpType
ACT = mybir.ActivationFunctionType
AX = mybir.AxisListType

IMAGES, SIDE, C = 32, 56, 96
WIN, SHIFT, HEADS = 7, 3, 12
L = WIN * WIN
D = C // HEADS
UNITS = SIDE // WIN
PAIRS = SIDE // WIN // 2
STEPS = UNITS * PAIRS
TOK = UNITS * L
HQ = 4
HG = HEADS // HQ
HP = HEADS // 2
HALF = HEADS // 2 * L
SC = HEADS * L
VC = 2 * 2 * (D + 1)
PW = 64
LEFT = 2
GRP = 3
EPS = 1e-5
TINY = 1e-36

QK_AT = {2: 4, 5: 5, 13: 6, 15: 7}
NEXT_QK_AT = {22: 0, 25: 1, 27: 2, 30: 3}
LATE = (5, 13, 15, 22, 25, 27, 30)
V_AT = {3: 1, 6: 2, 10: 3, 14: 4, 19: 5, 23: 6, 26: 7}
NEXT_V_STEP = 31
FILL_AT = {1: 6, 6: 7}
NEXT_FILL_AT = {13: 0, 14: 1, 17: 2, 22: 3, 24: 4, 29: 5}
EARLY_AT = {8: 3, 10: 4, 12: 5, 16: 6, 18: 7}
BOX_AT = {8: 0, 10: 1, 13: 2, 15: 3, 19: 4, 22: 5, 25: 6, 27: 7}
RESULT_AT = {12: 0, 16: 1, 18: 2, 19: 3, 22: 4, 26: 5, 28: 6, 30: 7}
NORM1_STEP, NORM2_STEP = 20, 6
FOLD_V_STEP = 26
X1_STEP = 11
LATER, LAST = 0.5, 0.9

K_ID, K_ROLL, K_BAND, K_GRP = 0, 128, 240, 336
K_MASK = 432
K_HALF = K_MASK + 4 * L
K_N = K_HALF + 2


def shape_constants():
    k = np.zeros((128, K_N), np.float32)
    k[:, K_ID:K_ID + 128] = np.eye(128)
    for j in range(2 * SIDE):
        k[j // SIDE * SIDE + (j % SIDE + SHIFT) % SIDE, K_ROLL + j] = 1
    for c in range(C):
        k[max(0, c - 10):min(C, c + 10), K_BAND + c] = 1
        k[c // GRP * GRP:(c // GRP + 1) * GRP, K_GRP + c] = 1.0 / GRP
    t = np.arange(L)
    region = [t // WIN >= WIN - SHIFT, t % WIN >= WIN - SHIFT]
    for last_row in range(2):
        for last_col in range(2):
            for w in range(2):
                cut = np.zeros((L, L), bool)
                if last_row:
                    cut |= region[0][:, None] != region[0][None, :]
                if last_col and w == 1:
                    cut |= region[1][:, None] != region[1][None, :]
                at = K_MASK + (2 * last_row + last_col) * L
                k[64 * w:64 * w + L, at:at + L] = np.where(cut, -100.0, 0.0)
    for h in range(2):
        k[64 * h:64 * h + L, K_HALF + h] = 1
    return k


class Signal:

    def __init__(self, sem, per, first=0):
        self.sem, self.per, self.first = sem, per, first

    def at(self, image, k):
        return image * self.per + (self.first + k)

    def some(self, image, k):
        return not isinstance(image, int) or image * self.per + k > 0


def build(nc, x, wT, bias_row, pT, pb_row, flipped, consts, out):
    ctx = ExitStack()
    with ctx:
        def sb(name, shape, dt=F32):
            return ctx.enter_context(nc.sbuf_tensor(name, shape, dt))

        def psum(name, shape):
            return ctx.enter_context(nc.psum_tensor(name, shape, F32))

        def signal(name, per, first=0):
            return Signal(ctx.enter_context(nc.semaphore(name)), per, first)

        K = sb("K", [128, K_N])
        ident = K[:, K_ID:K_ID + 128]
        roll = K[:, K_ROLL:K_ROLL + 2 * SIDE]
        band = K[0:C, K_BAND:K_BAND + C]
        group = K[0:C, K_GRP:K_GRP + C]
        half_of = K[:, K_HALF:K_HALF + 2]
        WT = sb("WT", [C + 1, 3 * C])
        W32 = sb("W32", [C + 1, 3 * C])
        WH = sb("WH", [C + 1, 3 * C], BF16)
        WL = sb("WL", [C + 1, 3 * C], BF16)
        PT = sb("PT", [C + 1, C])
        table = [sb(f"table{i}", [128, SC]) for i in range(4)]

        LOADS = UNITS
        tok_in = [sb(f"tok_in{i}", [2 * SIDE, 4, C]) for i in range(LOADS)]
        X = sb("X", [C, UNITS * TOK])
        XH = sb("XH", [C + 1, UNITS * TOK + 16], BF16)
        XL = sb("XL", [C + 1, UNITS * TOK + 16], BF16)
        qn = [[sb(f"qn{p}{i}", [C, 2 * TOK], BF16) for i in range(2)] for p in "hl"]
        kn = [[sb(f"kn{p}{i}", [C, 2 * TOK], BF16) for i in range(2)] for p in "hl"]
        QS = [sb(f"QS{i}", [128, HG, 2 * TOK + 16], BF16) for i in range(2)]
        KS = sb("KS", [128, HG, 2 * TOK], BF16)
        KE = [sb(f"KE{i}", [128, HEADS, 2 * TOK], BF16) for i in range(2)]
        VH = [sb(f"VH{i}", [128, PAIRS * HP, 2, 2, D + 1], BF16) for i in range(2)]
        VL = [sb(f"VL{i}", [128, PAIRS * HP, 2, 2, D + 1], BF16) for i in range(2)]
        T = [sb(f"T{i}", [128, HEADS, 64]) for i in range(4)]
        MX = [sb(f"MX{i}", [128, HEADS]) for i in range(4)]
        P32 = [sb(f"P32{i}", [128, HEADS, L]) for i in range(2)]
        bias_raw = P32[0][:, :, :].rearrange("p h k -> p (h k)").rearrange("p (k h) -> p k h", h=HEADS)
        PRH = [sb(f"PRH{i}", [128, HEADS, 64], BF16) for i in range(4)]
        PRL = [sb(f"PRL{i}", [128, HEADS, 64], BF16) for i in range(4)]
        rden = sb("rden", [128, 2 * HP, 2, 2])
        O = [sb(f"O{i}", [128, PAIRS, C]) for i in range(2)]
        OT = sb("OT", [C + 1, TOK])
        X1 = sb("X1", [C, SIDE, PW])
        Y = [sb(f"Y{i}", [C, WIN, PW]) for i in range(2)]
        SQ = [sb(f"SQ{i}", [C, WIN, PW]) for i in range(2)]
        y2 = sb("y2", [C, WIN, PW])
        y4 = sb("y4", [C, WIN, PW])
        q2 = sb("q2", [C, WIN, PW])
        q4 = sb("q4", [C, WIN, PW])
        ybox = [sb(f"ybox{i}", [C, WIN, SIDE]) for i in range(2)]
        qbox = [sb(f"qbox{i}", [C, WIN, SIDE]) for i in range(2)]
        ybox2 = [sb(f"ybox2{i}", [C, WIN, SIDE]) for i in range(2)]
        dent = sb("dent", [C, TOK])
        numt = sb("numt", [C, TOK])
        rd0 = [sb(f"rd0{i}", [C, TOK]) for i in range(2)]
        res = [sb(f"res{i}", [C, TOK + SIDE]) for i in range(2)]
        tok_out = [sb(f"tok_out{i}", [2 * SIDE, 4, C]) for i in range(2)]
        stats = [sb(f"stats{i}", [C, UNITS, 6]) for i in range(2)]
        mv = [sb(f"mv{i}", [C, 2]) for i in range(2)]
        g = [sb(f"g{i}", [C, 14]) for i in range(2)]
        DEV, V2, VE, LN, R0, SQR, SQV, NW, RS, NB, RS5, NB5, MEAN, GATE = range(14)
        tiny = sb("tiny", [C, 1])

        pS = psum("pS", [128, 2, 512])
        pP = psum("pP", [128, 2, 512])
        pO = psum("pO", [128, 512])
        pM = [psum(f"pM{i}", [128, 512]) for i in range(3)]
        box_bank = [pM[b] for b in (1, 0, 0, 0, 1, 0, 0, 1)]
        norm_bank = (pM[0], pM[2])
        early_bank = dict(zip(EARLY_AT.values(), (pM[b] for b in (1, 2, 1, 1, 2))))

        consts_in = signal("consts_in", 0)
        bias_in = signal("bias_in", 0)
        pool_fills = signal("pool_fills", 0)
        dve_fills = signal("dve_fills", 0)
        ones_ended = signal("ones_ended", 0)
        dve_setup = signal("dve_setup", 0)
        loaded = [signal(f"loaded{i}", 32 if i < UNITS - 1 else 64) for i in range(LOADS)]
        k_stacked = signal("k_stacked", 16 * 3 * HG * UNITS // 2)
        staged = [signal(f"staged{i}", 16 * (3 * HG + HQ)) for i in range(UNITS // 2)]
        stored = [signal(f"stored{i}", (128, 160)[i], 16) for i in range(2)]
        xT_made = signal("xT_made", UNITS)
        x_kept = signal("x_kept", UNITS)
        xh_made = signal("xh_made", UNITS)
        xl_made = signal("xl_made", UNITS)
        early_made = signal("early_made", len(EARLY_AT))
        early_stats = signal("early_stats", len(EARLY_AT))
        x_stats = signal("x_stats", UNITS - len(EARLY_AT))
        q_made = signal("q_made", UNITS)
        k_made = signal("k_made", UNITS)
        qh_made = signal("qh_made", UNITS)
        ql_made = signal("ql_made", UNITS)
        kh_made = signal("kh_made", UNITS)
        kl_made = signal("kl_made", UNITS)
        v_made = signal("v_made", UNITS)
        vh_made = signal("vh_made", 2 * UNITS)
        vl_made = signal("vl_made", 2 * UNITS)
        scores_made = signal("scores_made", STEPS)
        biased = signal("biased", STEPS)
        maxed = signal("maxed", STEPS)
        shifted = signal("shifted", STEPS)
        turned = signal("turned", 2 * STEPS)
        p32_made = signal("p32_made", 2 * STEPS)
        ph_made = signal("ph_made", 2 * STEPS)
        pl_made = signal("pl_made", 2 * STEPS)
        pv_made = signal("pv_made", STEPS)
        rden_made = signal("rden_made", 2 * UNITS)
        o_made = signal("o_made", 4 * UNITS)
        oT_made = signal("oT_made", UNITS)
        o_kept = signal("o_kept", UNITS)
        proj_made = signal("proj_made", UNITS)
        x1_made = signal("x1_made", UNITS)
        x1_stats = signal("x1_stats", UNITS)
        wrapped = signal("wrapped", 1)
        norm_pe = [signal("norm1_pe", 3), signal("norm2_pe", 2)]
        norm_dve = [signal("norm1_dve", 16), signal("norm2_dve", 12)]
        norm_act = [signal("norm1_act", 2), signal("norm2_act", 2)]
        y_made = signal("y_made", UNITS)
        sq_made = signal("sq_made", UNITS)
        ybox_step = signal("ybox_step", 3 * UNITS)
        qbox_step = signal("qbox_step", 5 * UNITS)
        ybox2_made = signal("ybox2_made", UNITS)
        den_made = signal("den_made", UNITS)
        num_made = signal("num_made", UNITS)
        den_kept = signal("den_kept", UNITS)
        num_kept = signal("num_kept", UNITS)
        ln_made = signal("ln_made", UNITS)
        rd0_made = signal("rd0_made", UNITS)
        ratio_step = signal("ratio_step", 4 * UNITS)
        resT_made = signal("resT_made", UNITS)
        tok_out_made = signal("tok_out_made", UNITS)

        def win_order(ap):
            return ap.rearrange("c (w i j) -> c i w j", w=UNITS, i=WIN)

        def image_rows(u, h2):
            tiles = 4 - h2
            first = WIN * u + h2 + SHIFT
            if u < UNITS - 1:
                return [(0, tiles, first)]
            return [(0, 2, first), (2, tiles - 2, first + 4 - SIDE)]

        def of_image(t, m):
            if isinstance(m, int):
                return t[m]
            return t[bass.ds(m, 1)].rearrange("n h w c -> (n h) w c")

        scores_operands = [KS, QS[0], QS[1], KE[0], KE[1]]
        block = ctx.enter_context(nc.Block())

        @block.sync
        def _(sp):
            def load(m, u):
                slot = u % LOADS
                if xT_made.some(m, u - LOADS + 1):
                    sp.wait_ge(xT_made.sem, xT_made.at(m, u - LOADS + 1))
                for h2 in range(2):
                    for t, n, row in image_rows(u, h2):
                        src = of_image(x, m)[row:row + 2 * n - 1:2, :, :].rearrange("t w c -> w t c")
                        sp.dma_start(tok_in[slot][SIDE * h2:SIDE * h2 + SIDE, t:t + n, :], src
                                     ).then_inc(loaded[slot].sem, 16)

            def value(v):
                return v if isinstance(v, int) else sp.to_reg(v)

            def stage(m, d):
                b = d % 2
                k_parts, q_parts = value(kl_made.at(m, 2 * d + 2)), value(ql_made.at(m, 2 * d + 2))
                spread = value(staged[d - 1].at(m + (d > 0), 0))
                used = None
                if scores_made.some(m, 2 * PAIRS * (d - 1)):
                    used = value(scores_made.at(m, 2 * PAIRS * (d - 1)))
                sp.wait_ge(kl_made.sem, k_parts)
                if staged[d - 1].some(m + (d > 0), 0):
                    sp.wait_ge(staged[d - 1].sem, spread)
                for r, part in enumerate((0, 0, 1)):
                    for gq in range(HG):
                        sp.dma_start(KS[r:128:4, gq, :], kn[part][b][32 * gq:32 * gq + 32, :]
                                     ).then_inc(k_stacked.sem, 16)
                sp.wait_ge(ql_made.sem, q_parts)
                if used is not None:
                    sp.wait_ge(scores_made.sem, used)
                for r, part in enumerate((0, 1, 0)):
                    for gq in range(HG):
                        sp.dma_start(QS[b][r:128:4, gq, 0:2 * TOK], qn[part][b][32 * gq:32 * gq + 32, :]
                                     ).then_inc(staged[d].sem, 16)
                sp.wait_ge(k_stacked.sem, k_stacked.at(m, 16 * 3 * HG * (d + 1)))
                for i in range(HQ):
                    rows = slice(32 * i, 32 * i + 32)
                    sp.dma_start(KE[b][rows, i::HQ, :], KS[rows, :, :]).then_inc(staged[d].sem, 16)

            def store(m, v):
                slot = v % 2
                sp.wait_ge(tok_out_made.sem, tok_out_made.at(m, v + 1))
                for h2 in range(2):
                    for t, n, row in image_rows(v, h2):
                        dst = of_image(out, m)[row:row + 2 * n - 1:2, :, :].rearrange("t w c -> w t c")
                        sp.dma_start(dst, tok_out[slot][SIDE * h2:SIDE * h2 + SIDE, t:t + n, :]
                                     ).then_inc(stored[slot].sem, 16)

            def image(n, own, last, more):
                if own:
                    stage(n, 1)
                if more and own:
                    for u in range(UNITS):
                        load(n + 1, u)
                if own:
                    stage(n, 2)
                if last:
                    store(n - 1, 0)
                if own:
                    stage(n, 3)
                if last:
                    for v in range(1, 5):
                        store(n - 1, v)
                if more:
                    stage(n + 1, 0)
                if last:
                    for v in range(5, UNITS):
                        store(n - 1, v)

            sp.dma_start(K[:, :], consts).then_inc(consts_in.sem, 16)
            for u in range(UNITS):
                load(0, u)
            sp.dma_start(WT[0:C, :], wT).then_inc(consts_in.sem, 16)
            sp.dma_start(WT[C:C + 1, :], bias_row).then_inc(consts_in.sem, 16)
            sp.dma_start(PT[0:C, :], pT).then_inc(consts_in.sem, 16)
            sp.dma_start(PT[C:C + 1, :], pb_row).then_inc(consts_in.sem, 16)
            for i in range(2):
                sp.dma_start(tok_out[i][0:1, 0, :], pb_row).then_inc(stored[i].sem, 16)
            sp.wait_ge(pool_fills.sem, 1)
            for q in range(L):
                i, j = q // WIN, q % WIN
                src = flipped[WIN - 1 - i:2 * WIN - 1 - i, WIN - 1 - j:2 * WIN - 1 - j, :]
                sp.dma_start(bias_raw[q:q + 65:64, :, :].rearrange("p (i j) h -> p i (j h)", i=WIN),
                             src.rearrange("(o i) j h -> o i (j h)", o=1).broadcast_to([2, WIN, WIN * HEADS])
                             ).then_inc(bias_in.sem, 16)
            sp.wait_ge(dve_fills.sem, len(scores_operands))

            image(-1, False, False, True)
            image(0, True, False, True)
            with sp.Fori(1, IMAGES - 1) as n:
                image(n, True, True, True)
            image(IMAGES - 1, True, True, False)
            image(IMAGES, False, True, False)
            for s in range(2):
                sp.wait_ge(stored[s].sem, stored[s].at(IMAGES, 0))

        @block.tensor
        def _(pe):
            reads = [[(j + LATER * (j in LATE), "own", s, u + 1) for j, u in QK_AT.items()]
                     + [(j + LATER * (j in LATE), "next", s, u + 1) for j, u in NEXT_QK_AT.items()]
                     for s in (ql_made, kl_made)]
            reads[0] += [(LAST, "last", x1_made, 7), (PAIRS + LAST, "last", x1_made, 8)]
            reads[0] += [(PAIRS * (u + 2) + LAST, "own", x1_made, u + 1) for u in range(UNITS - 2)]
            reads[1] += [(j + LATER, "own", vl_made, 2 * u + 2) for j, u in V_AT.items()]
            reads[0] += [(NORM1_STEP - LATER, "next", norm_dve[0], 2), (NORM1_STEP, "next", norm_dve[0], 5)]
            reads[1] += [(NORM1_STEP + 1 + LATER, "next", norm_dve[0], 12), (NEXT_V_STEP + LATER, "next", vl_made, 2)]
            reads.append([(j + LATER, "own", xh_made, u + 1) for j, u in FILL_AT.items()]
                         + [(j + LATER, "next", xh_made, u + 1) for j, u in NEXT_FILL_AT.items()]
                         + [(j + LAST, "last", tok_out_made, v + 1) for j, v in RESULT_AT.items()]
                         + [(PAIRS - 1 + LATER, "last", o_kept, UNITS)]
                         + [(PAIRS * u + 7 + LATER, "own", o_kept, u + 1) for u in range(UNITS - 1)])
            reads[2] += [(NORM2_STEP - LATER, "last", norm_dve[1], 2), (NORM2_STEP, "last", norm_dve[1], 5)]
            for i, (j, u) in enumerate(EARLY_AT.items()):
                reads[pM.index(early_bank[u])].append((j, "next", early_stats, i + 1))
            for j, v in BOX_AT.items():
                reads[pM.index(box_bank[v])] += [(j + 1 + LATER, "last", den_kept, v + 1),
                                                 (j + 2, "last", num_kept, v + 1)]
            reads = [sorted(r, key=lambda e: e[0]) for r in reads]

            def wait_for_bank(b, n, whose, at):
                before = [e for e in reads[b] if e[0] < at and e[1] in whose]
                image = {"last": n - 1, "own": n, "next": n + 1}
                if not before:
                    before = [e for e in reads[b] if e[1] == "own" and "last" in whose
                              or e[1] == "next" and "own" in whose]
                    image = {"own": n - 1, "next": n}
                if before:
                    _, kind, s, count = before[-1]
                    pe.wait_ge(s.sem, s.at(image[kind], count))

            def turn_x(m, u, bank, done):
                pe.wait_ge(loaded[u].sem, loaded[u].at(m + 1, 0))
                for t in range(4):
                    k = 2 * SIDE if t < 3 else SIDE
                    mm = pe.transpose(bank[0:C, 2 * SIDE * t:2 * SIDE * t + k], tok_in[u][0:k, t, :],
                                      roll[0:k, 0:k])
                mm.then_inc(done.sem, 1)

            def project(dst, col, u, done):
                xs = slice(TOK * u, TOK * u + TOK)
                pe.matmul(dst[0:C, 0:TOK], WH[:, col:col + C], XH[:, xs], start=True, stop=False)
                pe.matmul(dst[0:C, 0:TOK], WH[:, col:col + C], XL[:, xs], start=False, stop=False)
                pe.matmul(dst[0:C, 0:TOK], WL[:, col:col + C], XH[:, xs], start=False, stop=True
                          ).then_inc(done.sem, 1)

            def qk(m, u):
                if u == 0:
                    pe.wait_ge(norm_dve[0].sem, norm_dve[0].at(m, 14))
                pe.wait_ge(xl_made.sem, xl_made.at(m, u + 1))
                project(pM[0], 0, u, q_made)
                project(pM[1], C, u, k_made)

            def values(m, u):
                if u == 0:
                    pe.wait_ge(norm_dve[0].sem, norm_dve[0].at(m, 16))
                pe.wait_ge(xl_made.sem, xl_made.at(m, min(u + 2, UNITS)))
                for w in range(2):
                    for p in range(PAIRS):
                        at = TOK * u + L * (2 * p + w)
                        xh, xl = XH[:, at:at + 64], XL[:, at:at + 64]
                        col = (PAIRS * w + p) * C // 2
                        for part, (lhs, rhs) in enumerate(((xh, WH), (xh, WL), (xl, WH))):
                            for h in range(2):
                                wv = rhs[:, 2 * C:3 * C].rearrange("c (a h d) -> c a h d", h=2, d=D)
                                mm = pe.matmul(pM[1][64 * h:64 * h + 64, col:col + C // 2], lhs, wv[:, :, h, :],
                                               start=(part == 0), stop=(part == 2))
                mm.then_inc(v_made.sem, 1)

            def scores(m, j):
                u, p = divmod(j, PAIRS)
                if j % (2 * PAIRS) == 0:
                    pe.wait_ge(staged[u // 2].sem, staged[u // 2].at(m + 1, 0))
                if biased.some(m, j):
                    pe.wait_ge(biased.sem, biased.at(m, j))
                Q, E = QS[u // 2 % 2], KE[u // 2 % 2]
                for w in range(2):
                    at = TOK * (u % 2) + L * (2 * p + w)
                    for gq, h0, h1 in ((0, 0, 4), (1, 4, 6), (1, 6, 8), (2, 8, 12)):
                        bank, col = divmod(h0 * L, HALF)
                        mm = pe.matmul(pS[64 * w:64 * w + 64, bank, col:col + (h1 - h0) * L],
                                       Q[:, gq, at:at + 64], E[:, h0:h1, at:at + L], start=True, stop=True)
                mm.then_inc(scores_made.sem, 1)

            def turn_scores(m, j):
                pe.wait_ge(shifted.sem, shifted.at(m, j + 1))
                for c in range(2):
                    if ph_made.some(m, 2 * j - 1 + c):
                        pe.wait_ge(ph_made.sem, ph_made.at(m, 2 * j - 1 + c))
                    for h in range(3):
                        h0 = 2 * (3 * c + h)
                        mm = pe.transpose(pP[:, c, 128 * h:128 * h + 128], T[j % 4][:, h0:h0 + 2, :], ident)
                    mm.then_inc(turned.sem, 1)

            def times_v(m, j):
                u, p = divmod(j, PAIRS)
                pe.wait_ge(pl_made.sem, pl_made.at(m, 2 * j + 2))
                if p == 0:
                    pe.wait_ge(vl_made.sem, vl_made.at(m, 2 * u + 2))
                if p % 2 == 0 and o_made.some(m, j):
                    pe.wait_ge(o_made.sem, o_made.at(m, j))
                for h in range(HP):
                    dst = pO[:, VC * (HP * (p % 2) + h):VC * (HP * (p % 2) + h + 1)]
                    pr_h = PRH[j % 4][:, 2 * h:2 * h + 2, :]
                    pr_l = PRL[j % 4][:, 2 * h:2 * h + 2, :]
                    v_h = VH[u % 2][:, HP * p + h, :, :, :]
                    v_l = VL[u % 2][:, HP * p + h, :, :, :]
                    pe.matmul(dst, pr_h, v_h, start=True, stop=False)
                    pe.matmul(dst, pr_h, v_l, start=False, stop=False)
                    mm = pe.matmul(dst, pr_l, v_h, start=False, stop=True)
                mm.then_inc(pv_made.sem, 1)

            def turn_o(m, u):
                pe.wait_ge(o_made.sem, o_made.at(m, 4 * u + 4))
                for p in range(PAIRS):
                    mm = pe.transpose(pM[2][0:C, 128 * p:128 * p + 128], O[u % 2][:, p, :], ident)
                mm.then_inc(oT_made.sem, 1)

            def project_o(m, u):
                pe.wait_ge(o_kept.sem, o_kept.at(m, u + 1))
                dst = pM[0][0:C, 0:TOK]
                pe.matmul(dst, PT[:, :], OT[:, :], start=True, stop=False)
                pe.matmul(dst, ident[0:C, 0:C], X[:, TOK * u:TOK * u + TOK], start=False, stop=True
                          ).then_inc(proj_made.sem, 1)

            def norm_mean(m, which):
                pe.wait_ge(norm_dve[which].sem, norm_dve[which].at(m, 1))
                pe.matmul(norm_bank[which][0:C, 0:1], group, mv[which][:, 0:1], start=True, stop=True
                          ).then_inc(norm_pe[which].sem, 1)

            def norm_variance(m, which):
                pe.wait_ge(norm_dve[which].sem, norm_dve[which].at(m, 4))
                pe.matmul(norm_bank[which][0:C, 1:2], group, g[which][:, V2:V2 + 1], start=True, stop=True
                          ).then_inc(norm_pe[which].sem, 1)

            def norm_bias(m):
                pe.wait_ge(norm_dve[0].sem, norm_dve[0].at(m, 10))
                pe.matmul(pM[1][C:C + 1, 0:3 * C], g[0][:, NB:NB + 1], WT[0:C, :], start=True, stop=True
                          ).then_inc(norm_pe[0].sem, 1)

            def square_sums(m, v):
                pe.wait_ge(qbox_step.sem, qbox_step.at(m, 5 * v + 5))
                pe.matmul(box_bank[v][0:C, 0:TOK], band, qbox[v % 2][:, :, :], start=True, stop=True
                          ).then_inc(den_made.sem, 1)

            def box_squares(m, v):
                pe.wait_ge(ybox2_made.sem, ybox2_made.at(m, v + 1))
                pe.matmul(box_bank[v][0:C, 0:TOK], band, ybox2[v % 2][:, :, :], start=True, stop=True
                          ).then_inc(num_made.sem, 1)

            def turn_result(m, v):
                pe.wait_ge(ratio_step.sem, ratio_step.at(m, 4 * v + 4))
                for t in range(4):
                    mm = pe.transpose(pM[2][0:2 * SIDE, C * t:C * t + C],
                                      res[v % 2][:, 2 * SIDE * t:2 * SIDE * t + 2 * SIDE], ident[0:C, 0:C])
                mm.then_inc(resT_made.sem, 1)

            def image(n, own, last, more):
                whose = [w for w, there in (("own", own), ("last", last), ("next", more)) if there]
                for j in range(STEPS):
                    u, p = divmod(j, PAIRS)
                    if own and j + 1 < STEPS:
                        scores(n, j + 1)
                    if more and j + 1 == STEPS:
                        scores(n + 1, 0)
                    if (last if j < 3 else own):
                        times_v(*((n, j - 3) if j >= 3 else (n - 1, STEPS + j - 3)))
                    if own and j in QK_AT and j not in LATE:
                        wait_for_bank(0, n, whose, j)
                        wait_for_bank(1, n, whose, j)
                        qk(n, QK_AT[j])
                    if more and j in NEXT_QK_AT and j not in LATE:
                        wait_for_bank(0, n, whose, j)
                        wait_for_bank(1, n, whose, j)
                        qk(n + 1, NEXT_QK_AT[j])
                    if last and j - 2 in BOX_AT:
                        v = BOX_AT[j - 2]
                        wait_for_bank(pM.index(box_bank[v]), n, whose, j)
                        box_squares(n - 1, v)
                    if more and j in EARLY_AT:
                        bank = early_bank[EARLY_AT[j]]
                        wait_for_bank(pM.index(bank), n, whose, j)
                        turn_x(n + 1, EARLY_AT[j], bank, early_made)
                    if more and j == NORM1_STEP:
                        wait_for_bank(0, n, whose, j)
                        norm_variance(n + 1, 0)
                    if last and j == NORM2_STEP:
                        wait_for_bank(2, n, whose, j)
                        norm_variance(n - 1, 1)
                    if (own if j else last):
                        turn_scores(*((n, j - 1) if j else (n - 1, STEPS - 1)))
                    if p == 3 and (last if u == 0 else own):
                        wait_for_bank(2, n, whose, j + LATER)
                        turn_o(*((n, u - 1) if u else (n - 1, UNITS - 1)))
                    if last and j - 1 in BOX_AT:
                        v = BOX_AT[j - 1]
                        wait_for_bank(pM.index(box_bank[v]), n, whose, j + LATER)
                        square_sums(n - 1, v)
                    if more and j + 1 == NORM1_STEP:
                        wait_for_bank(0, n, whose, j + LATER)
                        norm_mean(n + 1, 0)
                    if last and j + 1 == NORM2_STEP:
                        wait_for_bank(2, n, whose, j + LATER)
                        norm_mean(n - 1, 1)
                    if more and j == NORM1_STEP + 1:
                        wait_for_bank(1, n, whose, j + LATER)
                        norm_bias(n + 1)
                    if own and j in QK_AT and j in LATE:
                        wait_for_bank(0, n, whose, j + LATER)
                        wait_for_bank(1, n, whose, j + LATER)
                        qk(n, QK_AT[j])
                    if more and j in NEXT_QK_AT and j in LATE:
                        wait_for_bank(0, n, whose, j + LATER)
                        wait_for_bank(1, n, whose, j + LATER)
                        qk(n + 1, NEXT_QK_AT[j])
                    if own and j in FILL_AT:
                        wait_for_bank(2, n, whose, j + LATER)
                        turn_x(n, FILL_AT[j], pM[2], xT_made)
                    if more and j in NEXT_FILL_AT:
                        wait_for_bank(2, n, whose, j + LATER)
                        turn_x(n + 1, NEXT_FILL_AT[j], pM[2], xT_made)
                    if own and j in V_AT:
                        wait_for_bank(1, n, whose, j + LATER)
                        values(n, V_AT[j])
                    if more and j == NEXT_V_STEP:
                        wait_for_bank(1, n, whose, j + LATER)
                        values(n + 1, 0)
                    if last and j in RESULT_AT:
                        wait_for_bank(2, n, whose, j + LAST)
                        turn_result(n - 1, RESULT_AT[j])
                    if p == 0 and (last if u < 2 else own):
                        wait_for_bank(0, n, whose, j + LAST)
                        project_o(*((n, u - 2) if u >= 2 else (n - 1, UNITS + u - 2)))

            pe.wait_ge(consts_in.sem, 16 * 5)
            image(-1, False, False, True)
            image(0, True, False, True)
            with pe.Fori(1, IMAGES - 1) as n:
                image(n, True, True, True)
            image(IMAGES - 1, True, True, False)
            image(IMAGES, False, True, False)

        @block.scalar
        def _(act):
            act.preload_act_table_set("natural_log_exp_and_others")

            def keep_x(m, u):
                act.wait_ge(xT_made.sem, xT_made.at(m, u + 1))
                if proj_made.some(m - 1, u + 1):
                    act.wait_ge(proj_made.sem, proj_made.at(m - 1, u + 1))
                src = pM[2][0:C, 0:TOK].rearrange("c (i w j) -> c i w j", i=WIN, w=UNITS)
                act.activation(win_order(X[:, TOK * u:TOK * u + TOK]), src, ACT.Copy).then_inc(x_kept.sem, 1)
                act.activation(win_order(XH[0:C, TOK * u:TOK * u + TOK]), src, ACT.Copy
                               ).then_inc(xh_made.sem, 1)

            def high_qk(m, u):
                act.wait_ge(q_made.sem, q_made.at(m, u + 1))
                last, b, s = u // 2 - 2, u // 2 % 2, slice(TOK * (u % 2), TOK * (u % 2) + TOK)
                if staged[last].some(m + (last >= 0), 0):
                    act.wait_ge(staged[last].sem, staged[last].at(m + (last >= 0), 0))
                act.activation(qn[0][b][:, s], pM[0][0:C, 0:TOK], ACT.Copy).then_inc(qh_made.sem, 1)
                act.wait_ge(k_made.sem, k_made.at(m, u + 1))
                act.activation(kn[0][b][:, s], pM[1][0:C, 0:TOK], ACT.Copy).then_inc(kh_made.sem, 1)

            def high_v(m, u):
                act.wait_ge(v_made.sem, v_made.at(m, u + 1))
                if pv_made.some(m, PAIRS * (u - 1)):
                    act.wait_ge(pv_made.sem, pv_made.at(m, PAIRS * (u - 1)))
                for h in range(2):
                    ps = slice(64 * h, 64 * h + L)
                    act.activation(VH[u % 2][ps, :, :, h, 0:D].rearrange("p a w d -> p w a d"),
                                   pM[1][ps, 0:PAIRS * C].rearrange("p (w a d) -> p w a d", w=2, d=D), ACT.Copy
                                   ).then_inc(vh_made.sem, 1)

            def exponentials(m, j):
                for c in range(2):
                    act.wait_ge(turned.sem, turned.at(m, 2 * j + c + 1))
                    if pl_made.some(m, 2 * (j - 2) + c + 1):
                        act.wait_ge(pl_made.sem, pl_made.at(m, 2 * (j - 2) + c + 1))
                    src = pP[:, c, 0:6 * 64].rearrange("p (a q) -> p a q", q=64)[:, :, 0:L]
                    act.activation(P32[j % 2][:, 6 * c:6 * c + 6, :], src, ACT.Exp).then_inc(p32_made.sem, 1)
                    if pv_made.some(m, j - 3):
                        act.wait_ge(pv_made.sem, pv_made.at(m, j - 3))
                    act.activation(PRH[j % 4][:, 6 * c:6 * c + 6, 0:L], src, ACT.Exp).then_inc(ph_made.sem, 1)

            def keep_o(m, u):
                act.wait_ge(oT_made.sem, oT_made.at(m, u + 1))
                if proj_made.some(m, u):
                    act.wait_ge(proj_made.sem, proj_made.at(m, u))
                src = pM[2][0:C, :].rearrange("c (a q) -> c a q", q=64)[:, :, 0:L]
                act.activation(OT[0:C, :].rearrange("c (a q) -> c a q", q=L), src, ACT.Copy
                               ).then_inc(o_kept.sem, 1)

            def keep_x1(m, u):
                act.wait_ge(proj_made.sem, proj_made.at(m, u + 1))
                if u < UNITS - 2 and ratio_step.some(m - 1, 4 * u + 4):
                    act.wait_ge(ratio_step.sem, ratio_step.at(m - 1, 4 * u + 4))
                at = LEFT + SHIFT
                dst = X1[:, WIN * u:WIN * u + WIN, at:at + SIDE].rearrange("c i (w j) -> c i w j", j=WIN)
                src = pM[0][0:C, 0:TOK].rearrange("c (w i j) -> c i w j", w=UNITS, i=WIN)
                act.activation(dst, src, ACT.Copy).then_inc(x1_made.sem, 1)

            def norm_root(m, which):
                gw = g[which]
                s = norm_act[which]
                act.wait_ge(norm_dve[which].sem, norm_dve[which].at(m, 5))
                act.activation(gw[:, LN:LN + 1], gw[:, VE:VE + 1], ACT.Ln).then_inc(s.sem, 1)
                act.wait_ge(s.sem, s.at(m, 1))
                act.activation(gw[:, R0:R0 + 1], gw[:, LN:LN + 1], ACT.Exp, scale=-0.5).then_inc(s.sem, 1)

            def normalise(m, v):
                if v == 0:
                    act.wait_ge(norm_dve[1].sem, norm_dve[1].at(m, 12))
                    act.wait_ge(wrapped.sem, wrapped.at(m, 1))
                rows = slice(WIN * v, WIN * v + WIN)
                cols = slice(LEFT, LEFT + SIDE)
                if v >= 2:
                    act.wait_ge(ybox_step.sem, ybox_step.at(m, 3 * (v - 1)))
                act.activation(Y[v % 2][:, :, cols], X1[:, rows, cols], ACT.Identity,
                               bias=g[1][:, NB:NB + 1], scale=g[1][:, RS:RS + 1]).then_inc(y_made.sem, 1)
                if v >= 2:
                    act.wait_ge(qbox_step.sem, qbox_step.at(m, 5 * (v - 2) + 3))
                act.activation(SQ[v % 2][:, :, cols], X1[:, rows, cols], ACT.Square,
                               bias=g[1][:, NB5:NB5 + 1], scale=g[1][:, RS5:RS5 + 1]).then_inc(sq_made.sem, 1)

            def square_box(m, v):
                act.wait_ge(ybox_step.sem, ybox_step.at(m, 3 * v + 3))
                if v >= 2:
                    act.wait_ge(num_made.sem, num_made.at(m, v - 1))
                act.activation(ybox2[v % 2][:, :, :], ybox[v % 2][:, :, :], ACT.Square
                               ).then_inc(ybox2_made.sem, 1)

            def keep_squares(m, v):
                act.wait_ge(den_made.sem, den_made.at(m, v + 1))
                if v:
                    act.wait_ge(ratio_step.sem, ratio_step.at(m, 4 * v - 1))
                act.activation(dent[:, :], box_bank[v][0:C, 0:TOK], ACT.Identity, bias=tiny[:, 0:1]
                               ).then_inc(den_kept.sem, 1)

            def keep_boxes(m, v):
                act.wait_ge(num_made.sem, num_made.at(m, v + 1))
                if v:
                    act.wait_ge(ratio_step.sem, ratio_step.at(m, 4 * v))
                act.activation(numt[:, :], box_bank[v][0:C, 0:TOK], ACT.Identity, bias=tiny[:, 0:1]
                               ).then_inc(num_kept.sem, 1)

            def invert(m, v):
                act.wait_ge(den_kept.sem, den_kept.at(m, v + 1))
                if v >= 2:
                    act.wait_ge(ratio_step.sem, ratio_step.at(m, 4 * (v - 2) + 2))
                act.activation(rd0[v % 2][:, :], dent[:, :], ACT.Ln).then_inc(ln_made.sem, 1)
                act.wait_ge(ln_made.sem, ln_made.at(m, v + 1))
                act.activation(rd0[v % 2][:, :], rd0[v % 2][:, :], ACT.Exp, scale=-1.0).then_inc(rd0_made.sem, 1)

            def keep_result(m, v):
                act.wait_ge(resT_made.sem, resT_made.at(m, v + 1))
                slot = v % 2
                act.wait_ge(stored[slot].sem, stored[slot].at(m, 32 * (v // 2)))
                act.activation(tok_out[slot][:, :, :].rearrange("p t c -> p (t c)"),
                               pM[2][0:2 * SIDE, 0:4 * C], ACT.Copy).then_inc(tok_out_made.sem, 1)

            def image(n, own, last, more):
                for j in range(STEPS):
                    u, p = divmod(j, PAIRS)
                    if own and j in QK_AT and j not in LATE:
                        high_qk(n, QK_AT[j])
                    if more and j in NEXT_QK_AT and j not in LATE:
                        high_qk(n + 1, NEXT_QK_AT[j])
                    if p == 1 and u >= 3 and own:
                        keep_x1(n, u - 2)
                    if p == 1 and u < 2 and last:
                        keep_x1(n - 1, UNITS + u - 2)
                    if last and j - 2 in BOX_AT:
                        keep_boxes(n - 1, BOX_AT[j - 2])
                    if (own if j else last):
                        exponentials(*((n, j - 1) if j else (n - 1, STEPS - 1)))
                    if p == 3 and (last if u == 0 else own):
                        keep_o(*((n, u - 1) if u else (n - 1, UNITS - 1)))
                    if j == X1_STEP and own:
                        keep_x1(n, 0)
                    if last and j - 1 in BOX_AT:
                        square_box(n - 1, BOX_AT[j - 1])
                        keep_squares(n - 1, BOX_AT[j - 1])
                    if more and j == NORM1_STEP:
                        norm_root(n + 1, 0)
                    if last and j == NORM2_STEP:
                        norm_root(n - 1, 1)
                    if own and j in QK_AT and j in LATE:
                        high_qk(n, QK_AT[j])
                    if more and j in NEXT_QK_AT and j in LATE:
                        high_qk(n + 1, NEXT_QK_AT[j])
                    if own and j in FILL_AT:
                        keep_x(n, FILL_AT[j])
                    if more and j in NEXT_FILL_AT:
                        keep_x(n + 1, NEXT_FILL_AT[j])
                    if own and j in V_AT:
                        high_v(n, V_AT[j])
                    if more and j == NEXT_V_STEP:
                        high_v(n + 1, 0)
                    if last and j - 1 in BOX_AT:
                        invert(n - 1, BOX_AT[j - 1])
                    if last and j + 1 in BOX_AT:
                        normalise(n - 1, BOX_AT[j + 1])
                    if last and j in RESULT_AT:
                        keep_result(n - 1, RESULT_AT[j])

            act.wait_ge(ones_ended.sem, 1)
            image(-1, False, False, True)
            image(0, True, False, True)
            with act.Fori(1, IMAGES - 1) as n:
                image(n, True, True, True)
            image(IMAGES - 1, True, True, False)
            image(IMAGES, False, True, False)

        @block.vector
        def _(dve):
            def add_bias(m, j):
                u, p = divmod(j, PAIRS)
                dve.wait_ge(scores_made.sem, scores_made.at(m, j + 1))
                if turned.some(m, 2 * (j - 3)):
                    dve.wait_ge(turned.sem, turned.at(m, 2 * (j - 3)))
                tab = table[2 * (u == UNITS - 1) + (p == PAIRS - 1)]
                dve.tensor_tensor(T[j % 4][:, :, 0:L].rearrange("p (b h) k -> p b h k", b=2),
                                  pS[:, :, 0:HALF].rearrange("p b (h k) -> p b h k", k=L),
                                  tab[:, :].rearrange("p (b h k) -> p b h k", b=2, k=L), ALU.add
                                  ).then_inc(biased.sem, 1)

            def maximum(m, j):
                dve.wait_ge(biased.sem, biased.at(m, j + 1))
                dve.tensor_reduce(MX[j % 4][:, :], T[j % 4][:, :, 0:L],
                                  AX.X, ALU.max).then_inc(maxed.sem, 1)

            def low_qk(m, u):
                dve.wait_ge(qh_made.sem, qh_made.at(m, u + 1))
                b, s = u // 2 % 2, slice(TOK * (u % 2), TOK * (u % 2) + TOK)
                dve.tensor_tensor(qn[1][b][:, s], pM[0][0:C, 0:TOK], qn[0][b][:, s], ALU.subtract
                                  ).then_inc(ql_made.sem, 1)
                dve.wait_ge(kh_made.sem, kh_made.at(m, u + 1))
                dve.tensor_tensor(kn[1][b][:, s], pM[1][0:C, 0:TOK], kn[0][b][:, s], ALU.subtract
                                  ).then_inc(kl_made.sem, 1)

            def low_v(m, u):
                for h in range(2):
                    ps = slice(64 * h, 64 * h + L)
                    dve.wait_ge(vh_made.sem, vh_made.at(m, 2 * u + h + 1))
                    dve.tensor_tensor(VL[u % 2][ps, :, :, h, 0:D].rearrange("p a w d -> p w a d"),
                                      pM[1][ps, 0:PAIRS * C].rearrange("p (w a d) -> p w a d", w=2, d=D),
                                      VH[u % 2][ps, :, :, h, 0:D].rearrange("p a w d -> p w a d"), ALU.subtract
                                      ).then_inc(vl_made.sem, 1)

            got = pO[:, 0:2 * HP * VC].rearrange("p (a w h d) -> p a w h d", w=2, h=2, d=D + 1)

            def invert_sums(m, u, half):
                dve.wait_ge(pv_made.sem, pv_made.at(m, PAIRS * u + 2 * half + 2))
                if o_made.some(m, 4 * u + 2 * half):
                    dve.wait_ge(o_made.sem, o_made.at(m, 4 * u + 2 * half))
                dve.reciprocal(rden[:, :, :, :], got[:, :, :, :, D]).then_inc(rden_made.sem, 1)

            def divide_o(m, u, half):
                dve.wait_ge(rden_made.sem, rden_made.at(m, 2 * u + half + 1))
                if oT_made.some(m, u - 1):
                    dve.wait_ge(oT_made.sem, oT_made.at(m, u - 1))
                for w in range(2):
                    ps = slice(64 * w, 64 * w + 64)
                    dst = O[u % 2][ps, 2 * half:2 * half + 2, :].rearrange("p a (b h d) -> p (a b) h d", h=2, d=D)
                    by = rden[ps, :, w, :].unsqueeze(3).broadcast_to([64, 2 * HP, 2, D])
                    dve.tensor_tensor(dst, got[ps, :, w, :, 0:D], by, ALU.mult).then_inc(o_made.sem, 1)

            def stats_of_x1(m, u):
                at = LEFT + SHIFT
                dve.wait_ge(x1_made.sem, x1_made.at(m, u + 1))
                dve.bn_stats(stats[1][:, u, :], X1[:, WIN * u:WIN * u + WIN, at:at + SIDE]
                             ).then_inc(x1_stats.sem, 1)

            def stats_of_x(m, u):
                dve.wait_ge(x_kept.sem, x_kept.at(m, u + 1))
                dve.bn_stats(stats[0][:, u, :], X[:, TOK * u:TOK * u + TOK]).then_inc(x_stats.sem, 1)

            def early_stats_of_x(m, k, u):
                dve.wait_ge(early_made.sem, early_made.at(m, k + 1))
                dve.bn_stats(stats[0][:, u, :], early_bank[u][0:C, 0:TOK]).then_inc(early_stats.sem, 1)

            def norm_link(m, which, k, ins):
                ins.then_inc(norm_dve[which].sem, 1)
                dve.wait_ge(norm_dve[which].sem, norm_dve[which].at(m, k))

            def norm_mean(m, which):
                if which:
                    dve.wait_ge(x1_stats.sem, x1_stats.at(m, UNITS))
                else:
                    dve.wait_ge(x_stats.sem, x_stats.at(m + 1, 0))
                    dve.wait_ge(early_stats.sem, early_stats.at(m + 1, 0))
                dve.memset(g[which][:, GATE:GATE + 1], 0.0)
                norm_link(m, which, 1, dve.bn_aggr(mv[which][:, :], stats[which][:, :, :].rearrange("c u s -> c (u s)")))

            def norm_deviation(m, which):
                gw, mw = g[which], mv[which]
                dve.wait_ge(norm_pe[which].sem, norm_pe[which].at(m, 1))
                norm_link(m, which, 2, dve.tensor_copy(gw[:, MEAN:MEAN + 1], norm_bank[which][0:C, 0:1]))
                norm_link(m, which, 3, dve.tensor_tensor(gw[:, DEV:DEV + 1], mw[:, 0:1], gw[:, MEAN:MEAN + 1],
                                                         ALU.subtract))
                norm_link(m, which, 4, dve.scalar_tensor_tensor(
                    out=gw[:, V2:V2 + 1], in0=gw[:, DEV:DEV + 1], scalar=gw[:, DEV:DEV + 1], in1=mw[:, 1:2],
                    op0=ALU.mult, op1=ALU.add))

            def norm_variance(m, which):
                dve.wait_ge(norm_pe[which].sem, norm_pe[which].at(m, 2))
                norm_link(m, which, 5, dve.tensor_scalar(g[which][:, VE:VE + 1], norm_bank[which][0:C, 1:2], EPS,
                                                         None, ALU.add))

            def norm_scale(m, which):
                gw = g[which]

                def col(i):
                    return gw[:, i:i + 1]

                dve.wait_ge(norm_act[which].sem, norm_act[which].at(m, 2))
                norm_link(m, which, 6, dve.tensor_tensor(col(SQR), col(R0), col(R0), ALU.mult))
                norm_link(m, which, 7, dve.tensor_tensor(col(SQV), col(SQR), col(VE), ALU.mult))
                norm_link(m, which, 8, dve.tensor_scalar(col(NW), col(SQV), -0.5, 1.5, ALU.mult, ALU.add))
                norm_link(m, which, 9, dve.tensor_tensor(col(RS), col(R0), col(NW), ALU.mult))
                norm_link(m, which, 10, dve.scalar_tensor_tensor(
                    out=col(NB), in0=col(MEAN), scalar=-1.0, in1=col(RS), op0=ALU.mult, op1=ALU.mult))
                if which:
                    norm_link(m, 1, 11, dve.tensor_scalar(col(RS5), col(RS), 5.0 ** 0.5, None, ALU.mult))
                    norm_link(m, 1, 12, dve.tensor_scalar(col(NB5), col(NB), 5.0 ** 0.5, None, ALU.mult))
                else:
                    norm_link(m, 0, 11, dve.tensor_scalar(W32[0:C, :], WT[0:C, :], col(RS), None, ALU.mult))

            def fold_qk(m):
                qk = slice(0, 2 * C)
                dve.wait_ge(norm_pe[0].sem, norm_pe[0].at(m, 3))
                norm_link(m, 0, 12, dve.tensor_tensor(W32[C:C + 1, :], pM[1][C:C + 1, 0:3 * C], WT[C:C + 1, :],
                                                      ALU.add))
                if k_made.some(m, 0):
                    dve.wait_ge(k_made.sem, k_made.at(m, 0))
                norm_link(m, 0, 13, dve.tensor_copy(WH[:, qk], W32[:, qk]))
                norm_link(m, 0, 14, dve.tensor_tensor(WL[:, qk], W32[:, qk], WH[:, qk], ALU.subtract))

            def fold_v(m):
                of_v = slice(2 * C, 3 * C)
                if v_made.some(m, 0):
                    dve.wait_ge(v_made.sem, v_made.at(m, 0))
                norm_link(m, 0, 15, dve.tensor_copy(WH[:, of_v], W32[:, of_v]))
                norm_link(m, 0, 16, dve.tensor_tensor(WL[:, of_v], W32[:, of_v], WH[:, of_v], ALU.subtract))

            def wrap(m):
                at = LEFT + SIDE
                dve.wait_ge(x1_made.sem, x1_made.at(m, UNITS))
                dve.tensor_copy(X1[:, :, LEFT:LEFT + SHIFT], X1[:, :, at:at + SHIFT]).then_inc(wrapped.sem, 1)

            def pairs_of_squares(m, v):
                s, k = SQ[v % 2], 5 * v
                dve.wait_ge(sq_made.sem, sq_made.at(m, v + 1))
                dve.tensor_tensor(q2[:, :, 0:59], s[:, :, 0:59], s[:, :, 1:60], ALU.add).then_inc(qbox_step.sem, 1)
                dve.wait_ge(qbox_step.sem, qbox_step.at(m, k + 1))
                dve.tensor_tensor(q4[:, :, 0:56], q2[:, :, 0:56], q2[:, :, 2:58], ALU.add
                                  ).then_inc(qbox_step.sem, 1)

            def box_of_squares(m, v):
                s, q, k = SQ[v % 2], qbox[v % 2], 5 * v
                if v >= 2:
                    dve.wait_ge(den_made.sem, den_made.at(m, v - 1))
                dve.wait_ge(qbox_step.sem, qbox_step.at(m, k + 2))
                dve.tensor_tensor(q[:, :, :], q4[:, :, 0:56], s[:, :, 4:60], ALU.add).then_inc(qbox_step.sem, 1)
                dve.wait_ge(qbox_step.sem, qbox_step.at(m, k + 3))
                dve.tensor_scalar(q[:, :, 0:56:55], q[:, :, 0:56:55], 0.6, None, ALU.mult
                                  ).then_inc(qbox_step.sem, 1)
                dve.tensor_scalar(q[:, :, 1:55:53], q[:, :, 1:55:53], 0.8, None, ALU.mult
                                  ).then_inc(qbox_step.sem, 1)

            def quotient(m, v):
                k, s = 4 * v, ratio_step
                dve.wait_ge(rd0_made.sem, rd0_made.at(m, v + 1))
                if v:
                    dve.wait_ge(s.sem, s.at(m, k))
                dve.tensor_tensor(dent[:, :], dent[:, :], rd0[v % 2][:, :], ALU.mult).then_inc(s.sem, 1)
                dve.wait_ge(num_kept.sem, num_kept.at(m, v + 1))
                dve.tensor_tensor(numt[:, :], numt[:, :], rd0[v % 2][:, :], ALU.mult).then_inc(s.sem, 1)

            def result(m, v):
                k, s = 4 * v, ratio_step
                dve.wait_ge(s.sem, s.at(m, k + 2))
                dve.scalar_tensor_tensor(out=numt[:, :], in0=dent[:, :], scalar=-2.0,
                                         in1=numt[:, :],
                                         op0=ALU.add, op1=ALU.mult).then_inc(s.sem, 1)
                dve.wait_ge(s.sem, s.at(m, k + 3))
                if v >= 2:
                    dve.wait_ge(resT_made.sem, resT_made.at(m, v - 1))
                dve.tensor_tensor(res[v % 2][:, 0:TOK].rearrange("c (i w) -> c i w", i=WIN),
                                  X1[:, WIN * v:WIN * v + WIN, LEFT:LEFT + SIDE],
                                  numt[:, :].rearrange("c (i w) -> c i w", i=WIN), ALU.subtract
                                  ).then_inc(s.sem, 1)

            def setup_link(k, ins):
                ins.then_inc(dve_setup.sem, 1)
                dve.wait_ge(dve_setup.sem, k)

            def make_tables():
                dve.wait_ge(bias_in.sem, 16 * L)
                setup_link(7, dve.tensor_copy(table[0][:, :].rearrange("p (h k) -> p h k", h=HEADS),
                                              bias_raw[:, :, :].rearrange("p k h -> p h k")))
                for i, t in enumerate((3, 2, 1, 0)):
                    mask = K[:, K_MASK + L * t:K_MASK + L * t + L].unsqueeze(1).broadcast_to([128, HEADS, L])
                    setup_link(8 + i, dve.tensor_tensor(
                        table[t][:, :].rearrange("p (h k) -> p h k", h=HEADS),
                        table[0][:, :].rearrange("p (h k) -> p h k", h=HEADS), mask, ALU.add))

            def image(n, own, last, more):
                for j in range(STEPS):
                    u, p = divmod(j, PAIRS)
                    if j + 1 == STEPS and not own and more:
                        make_tables()
                    if last and j == NORM2_STEP:
                        norm_deviation(n - 1, 1)
                    if more and j == NORM1_STEP:
                        norm_deviation(n + 1, 0)
                    if own and j - 1 in QK_AT and j - 1 in LATE:
                        low_qk(n, QK_AT[j - 1])
                    if more and j - 1 in NEXT_QK_AT and j - 1 in LATE:
                        low_qk(n + 1, NEXT_QK_AT[j - 1])
                    if more and j - 1 in EARLY_AT:
                        early_stats_of_x(n + 1, list(EARLY_AT).index(j - 1), EARLY_AT[j - 1])
                    if last and j - 1 in BOX_AT:
                        box_of_squares(n - 1, BOX_AT[j - 1])
                    if last and j - 3 in BOX_AT:
                        result(n - 1, BOX_AT[j - 3])
                    if last and j == NORM2_STEP + 1:
                        norm_scale(n - 1, 1)
                    if more and j == NORM1_STEP + 1:
                        norm_scale(n + 1, 0)
                    if more and j == NORM1_STEP + 2:
                        fold_qk(n + 1)
                    if own and j + 1 < STEPS:
                        add_bias(n, j + 1)
                    if more and j + 1 == STEPS:
                        add_bias(n + 1, 0)
                    if own and (j - 1 in V_AT or j == 0):
                        low_v(n, V_AT[j - 1] if j else 0)
                    if p % 2 == 0 and (last if u == 0 else own):
                        invert_sums(*((n, u - 1, p // 2) if u else (n - 1, UNITS - 1, p // 2)))
                    if own and j + 1 < STEPS:
                        maximum(n, j + 1)
                    if more and j + 1 == STEPS:
                        maximum(n + 1, 0)
                    if p % 2 == 0 and (last if u == 0 else own):
                        divide_o(*((n, u - 1, p // 2) if u else (n - 1, UNITS - 1, p // 2)))
                    if p == 1 and u >= 3 and own:
                        stats_of_x1(n, u - 2)
                    if j == X1_STEP + 1 and own:
                        stats_of_x1(n, 0)
                    if p == 1 and u < 2 and last:
                        stats_of_x1(n - 1, UNITS + u - 2)
                    if last and j == NORM2_STEP - 1:
                        wrap(n - 1)
                        norm_mean(n - 1, 1)
                    if more and j - 2 in NEXT_FILL_AT and NEXT_FILL_AT[j - 2] not in EARLY_AT.values():
                        stats_of_x(n + 1, NEXT_FILL_AT[j - 2])
                    if more and j == NORM1_STEP - 1:
                        norm_mean(n + 1, 0)
                    if own and j in QK_AT and j not in LATE:
                        low_qk(n, QK_AT[j])
                    if more and j in NEXT_QK_AT and j not in LATE:
                        low_qk(n + 1, NEXT_QK_AT[j])
                    if last and j == NORM2_STEP:
                        norm_variance(n - 1, 1)
                    if more and j == NORM1_STEP:
                        norm_variance(n + 1, 0)
                    if last and j - 2 in BOX_AT:
                        quotient(n - 1, BOX_AT[j - 2])
                    if last and j in BOX_AT:
                        pairs_of_squares(n - 1, BOX_AT[j])
                    if more and j == FOLD_V_STEP:
                        fold_v(n + 1)

            for t in scores_operands:
                dve.memset(t[tuple([slice(None)] * len(t.shape))], 0.0).then_inc(dve_fills.sem, 1)
            dve.wait_ge(consts_in.sem, 16 * 5)
            dve.wait_ge(ones_ended.sem, 1)
            dve.memset(tiny[:, :], TINY).then_inc(dve_setup.sem, 1)
            setup_link(2, dve.tensor_scalar(WT[:, 0:C], WT[:, 0:C], float(D) ** -0.5, None, ALU.mult))
            for b in range(2):
                for w in range(2):
                    setup_link(3 + 2 * b + w, dve.tensor_copy(
                        VH[b][:, :, w, :, D], half_of.unsqueeze(1).broadcast_to([128, PAIRS * HP, 2])))

            image(-1, False, False, True)
            image(0, True, False, True)
            with dve.Fori(1, IMAGES - 1) as n:
                image(n, True, True, True)
            image(IMAGES - 1, True, True, False)
            image(IMAGES, False, True, False)

        @block.gpsimd
        def _(pool):
            def low_x(m, u):
                pool.wait_ge(xh_made.sem, xh_made.at(m, u + 1))
                s = slice(TOK * u, TOK * u + TOK)
                pool.tensor_tensor(XL[0:C, s], X[:, s], XH[0:C, s], ALU.subtract).then_inc(xl_made.sem, 1)

            def shift(m, j):
                pool.wait_ge(maxed.sem, maxed.at(m, j + 1))
                t = T[j % 4][:, :, 0:L]
                pool.tensor_tensor(t, t, MX[j % 4][:, :].unsqueeze(2).broadcast_to([128, HEADS, L]),
                                   ALU.subtract).then_inc(shifted.sem, 1)

            def low_p(m, j):
                for c in range(2):
                    pool.wait_ge(ph_made.sem, ph_made.at(m, 2 * j + c + 1))
                    hs = slice(6 * c, 6 * c + 6)
                    pool.tensor_tensor(PRL[j % 4][:, hs, 0:L], P32[j % 2][:, hs, :], PRH[j % 4][:, hs, 0:L],
                                       ALU.subtract).then_inc(pl_made.sem, 1)

            def pairs_of_y(m, v):
                y = Y[v % 2]
                pool.wait_ge(y_made.sem, y_made.at(m, v + 1))
                pool.tensor_tensor(y2[:, :, 0:59], y[:, :, 0:59], y[:, :, 1:60], ALU.add).then_inc(ybox_step.sem, 1)
                pool.wait_ge(ybox_step.sem, ybox_step.at(m, 3 * v + 1))
                pool.tensor_tensor(y4[:, :, 0:56], y2[:, :, 0:56], y2[:, :, 2:58], ALU.add
                                   ).then_inc(ybox_step.sem, 1)

            def box(m, v):
                y = Y[v % 2]
                if v >= 2:
                    pool.wait_ge(ybox2_made.sem, ybox2_made.at(m, v - 1))
                pool.wait_ge(ybox_step.sem, ybox_step.at(m, 3 * v + 2))
                pool.tensor_tensor(ybox[v % 2][:, :, :], y4[:, :, 0:56], y[:, :, 4:60], ALU.add
                                   ).then_inc(ybox_step.sem, 1)

            def image(n, own, last, more):
                for j in range(STEPS):
                    if last and j - 1 in BOX_AT:
                        box(n - 1, BOX_AT[j - 1])
                    if (last if j < 2 else own):
                        low_p(*((n, j - 2) if j >= 2 else (n - 1, STEPS + j - 2)))
                    if own and j + 1 < STEPS:
                        shift(n, j + 1)
                    if more and j + 1 == STEPS:
                        shift(n + 1, 0)
                    if own and j in FILL_AT:
                        low_x(n, FILL_AT[j])
                    if more and j in NEXT_FILL_AT:
                        low_x(n + 1, NEXT_FILL_AT[j])
                    if last and j in BOX_AT:
                        pairs_of_y(n - 1, BOX_AT[j])
            zero = [P32[0], XL, VL[0], VL[1], VH[0], VH[1], Y[0], Y[1], SQ[0], SQ[1], T[0], T[1], T[2], T[3],
                    PRL[0], PRL[1], PRL[2], PRL[3], O[0], O[1], res[0], res[1], X1]
            one = [XH, OT, PRH[0], PRH[1], PRH[2], PRH[3]]
            for t in zero:
                pool.memset(t[tuple([slice(None)] * len(t.shape))], 0.0).then_inc(pool_fills.sem, 1)
            for t in one:
                pool.memset(t[tuple([slice(None)] * len(t.shape))], 1.0).then_inc(pool_fills.sem, 1)
            pool.wait_ge(pool_fills.sem, len(zero) + len(one))
            pool.memset(XH[0:C, UNITS * TOK:], 0.0).then_inc(ones_ended.sem, 1)

            image(-1, False, False, True)
            image(0, True, False, True)
            with pool.Fori(1, IMAGES - 1) as n:
                image(n, True, True, True)
            image(IMAGES - 1, True, True, False)
            image(IMAGES, False, True, False)


def kernel(x, L0_conv_qkv_w, L0_conv_qkv_b, L0_conv_proj_w, L0_conv_proj_b, L0_conv_rel_table):
    import concourse.bacc as bacc
    from concourse.bass_utils import run_bass_kernel_spmd

    side = 2 * WIN - 1
    arrays = {
        "x": np.ascontiguousarray(x),
        "wT": np.ascontiguousarray(np.asarray(L0_conv_qkv_w).T),
        "bias_row": np.ascontiguousarray(np.asarray(L0_conv_qkv_b).reshape(1, 3 * C)),
        "pT": np.ascontiguousarray(np.asarray(L0_conv_proj_w).T),
        "pb_row": np.ascontiguousarray(np.asarray(L0_conv_proj_b).reshape(1, C)),
        "flipped": np.ascontiguousarray(np.asarray(L0_conv_rel_table).reshape(side, side, HEADS)[::-1, ::-1]),
        "consts": shape_constants(),
    }
    nc = bacc.Bacc("TRN2", target_bir_lowering=False, num_devices=1)
    args = [nc.dram_tensor(k, a.shape, mybir.dt.from_np(a.dtype), kind="ExternalInput").ap()
            for k, a in arrays.items()]
    out = nc.dram_tensor("out", (IMAGES, SIDE, SIDE, C), F32, kind="ExternalOutput").ap()
    build(nc, *args, out)
    r = run_bass_kernel_spmd(nc, [arrays], core_ids=[0])
    return r.results[0]["out"]
```
